# Optimizing a Trainium2 kernel written in Bass

```python
import numpy as np
import jax
import jax.numpy as jnp

def _softmax(x, axis=-1):
    return jax.nn.softmax(x, axis=axis)

def _gelu(x):
    return jax.nn.gelu(x, approximate=True)

def _silu(x):
    return jax.nn.silu(x)

def _sigmoid(x):
    return jax.nn.sigmoid(x)

def _layernorm(x, axis=-1, eps=1e-05):
    m = jnp.mean(x, axis=axis, keepdims=True)
    v = jnp.var(x, axis=axis, keepdims=True)
    return (x - m) / jnp.sqrt(v + eps)

def _scatter_add(tgt, idx, src, axis=0):
    return tgt.at[idx].add(src)

def _segment_sum(src, seg, n):
    return jax.ops.segment_sum(src, seg, n)
kernel_name = 'mk_xattn_ffn_d1_seqx_r4_397407'

def setup_inputs(seed: int=0):
    np.random.seed(seed)
    _w = jnp.asarray

    def _rec_inputs():
        import jax
        import jax.numpy as jnp
        _rk = jax.random.key(seed)
        x = -0.0003929 + 0.9999 * jax.random.normal(jax.random.fold_in(_rk, 1), (4, 512, 256), jnp.float32)
        _lenS = 512 - jax.random.randint(jax.random.fold_in(_rk, 7), (4,), 0, max(1, 512 // 4) + 1, jnp.int32)
        _lenS2 = 512 - jax.random.randint(jax.random.fold_in(_rk, 8), (4,), 0, max(1, 512 // 4) + 1, jnp.int32)
        _ctx_1024P = jax.random.normal(jax.random.fold_in(_rk, 11), (4, 16, 256), jnp.float32)
        _ctx_1024c = jax.random.dirichlet(jax.random.fold_in(_rk, 511), 0.3 * jnp.ones((16,), jnp.float32), (4, 512))
        _ctx_1024t = jnp.einsum('bsk,bkd->bsd', _ctx_1024c, _ctx_1024P)
        _ctx_1024t = _ctx_1024t * jax.lax.rsqrt(jnp.mean(jnp.square(_ctx_1024t)) + 1e-12) * 0.953939
        ctx_1024 = 2.81802e-05 + 1.00001 * (_ctx_1024t + 0.3 * jax.random.normal(jax.random.fold_in(_rk, 611), (4, 512, 256), jnp.float32))
        _validS = jnp.arange(512)[None, :] < _lenS[:, None]
        _validS2 = jnp.arange(512)[None, :] < _lenS2[:, None]
        _causal = jnp.tril(jnp.ones((512, 512), dtype=bool))
        mask_BxS2_ff1 = jnp.where(jnp.ones((4, 512), dtype=bool), 1.0, 0.0).astype(jnp.float32)
        return (x, ctx_1024, mask_BxS2_ff1)
    x, ctx_1024, mask_BxS2_ff1 = _rec_inputs()

    def _L0_xattn_setup():
        import jax, jax.numpy as jnp
        import numpy as np
        D_MODEL = 256
        HEADS = 16
        DEPTH = D_MODEL // HEADS
        B, S = (4, 1024)
        EPS_K = 1e-06
        EPS_LN = 1e-06

        def _layernorm(x, g, b):
            m = jnp.mean(x, axis=-1, keepdims=True)
            var = jnp.var(x, axis=-1, keepdims=True)
            return (x - m) * jax.lax.rsqrt(var + EPS_LN) * g + b

        def _split_heads(x):
            bsz, sl, _ = x.shape
            return x.reshape(bsz, sl, HEADS, DEPTH).transpose(0, 2, 1, 3)
        key = jax.random.key(seed)
        ks = jax.random.split(key, 8)
        lecun = 1.0 / np.sqrt(D_MODEL)
        glorot = np.sqrt(2.0 / (D_MODEL + D_MODEL))
        return {'q': jax.random.normal(ks[0], (B, S, D_MODEL), jnp.float32), 'k': jax.random.normal(ks[1], (B, S, D_MODEL), jnp.float32), 'v': jax.random.normal(ks[2], (B, S, D_MODEL), jnp.float32), 'mask': jnp.ones((B, S), jnp.float32), 'wq': jax.random.normal(ks[3], (D_MODEL, D_MODEL), jnp.float32) * lecun, 'wk': jax.random.normal(ks[4], (D_MODEL, D_MODEL), jnp.float32) * lecun, 'wv': jax.random.normal(ks[5], (D_MODEL, D_MODEL), jnp.float32) * lecun, 'ln_gamma': jnp.ones((D_MODEL,), jnp.float32), 'ln_beta': jnp.zeros((D_MODEL,), jnp.float32), 'dense_w': jax.random.normal(ks[6], (D_MODEL, D_MODEL), jnp.float32) * glorot, 'dense_b': jnp.zeros((D_MODEL,), jnp.float32)}
    _L0_xattn_all = _L0_xattn_setup()
    _L0_xattn_in = {k: v for k, v in _L0_xattn_all.items() if k in ('wq', 'wk', 'wv', 'ln_gamma', 'ln_beta', 'dense_w', 'dense_b')}
    del _L0_xattn_all

    def _L0_ffn_setup():
        import jax, jax.numpy as jnp
        import numpy as np
        D_MODEL = 256
        NUM_EXPERTS = 8
        TOP_K = 2
        key = jax.random.key(seed)
        k_x, k_g, k_w1, k_w2 = jax.random.split(key, 4)
        B, S, D, E = (4, 512, D_MODEL, NUM_EXPERTS)
        s_in = 1.0 / np.sqrt(D)
        s_hid = 1.0 / np.sqrt(4 * D)
        return {'x': jax.random.normal(k_x, (B, S, D), dtype=jnp.float32), 'gate_w': jax.random.uniform(k_g, (E, D), jnp.float32, -s_in, s_in), 'w1': jax.random.uniform(k_w1, (E, 4 * D, D), jnp.float32, -s_in, s_in), 'w2': jax.random.uniform(k_w2, (E, D, 4 * D), jnp.float32, -s_hid, s_hid)}
    _L0_ffn_all = _L0_ffn_setup()
    _L0_ffn_in = {k: v for k, v in _L0_ffn_all.items() if k in ('gate_w', 'w1', 'w2')}
    del _L0_ffn_all
    return {'x': x, 'ctx_1024': ctx_1024, 'mask_BxS2_ff1': mask_BxS2_ff1, 'L0_xattn_wq': _L0_xattn_in['wq'], 'L0_xattn_wk': _L0_xattn_in['wk'], 'L0_xattn_wv': _L0_xattn_in['wv'], 'L0_xattn_ln_gamma': _L0_xattn_in['ln_gamma'], 'L0_xattn_ln_beta': _L0_xattn_in['ln_beta'], 'L0_xattn_dense_w': _L0_xattn_in['dense_w'], 'L0_xattn_dense_b': _L0_xattn_in['dense_b'], 'L0_ffn_gate_w': _L0_ffn_in['gate_w'], 'L0_ffn_w1': _L0_ffn_in['w1'], 'L0_ffn_w2': _L0_ffn_in['w2']}

def reference(x, ctx_1024, mask_BxS2_ff1, L0_xattn_wq, L0_xattn_wk, L0_xattn_wv, L0_xattn_ln_gamma, L0_xattn_ln_beta, L0_xattn_dense_w, L0_xattn_dense_b, L0_ffn_gate_w, L0_ffn_w1, L0_ffn_w2):
    import jax
    import jax.numpy as jnp

    def _L0_xattn_ref(q, k, v, mask, wq, wk, wv, ln_gamma, ln_beta, dense_w, dense_b):
        import jax, jax.numpy as jnp
        import numpy as np
        D_MODEL = 256
        HEADS = 16
        DEPTH = D_MODEL // HEADS
        B, S = (4, 1024)
        EPS_K = 1e-06
        EPS_LN = 1e-06

        def _layernorm(x, g, b):
            m = jnp.mean(x, axis=-1, keepdims=True)
            var = jnp.var(x, axis=-1, keepdims=True)
            return (x - m) * jax.lax.rsqrt(var + EPS_LN) * g + b

        def _split_heads(x):
            bsz, sl, _ = x.shape
            return x.reshape(bsz, sl, HEADS, DEPTH).transpose(0, 2, 1, 3)
        bsz = q.shape[0]
        em = mask[:, None, :, None]
        qh = _split_heads(_layernorm(q @ wq, ln_gamma, ln_beta))
        kh = _split_heads(_layernorm(k @ wk, ln_gamma, ln_beta))
        vh = _split_heads(_layernorm(v @ wv, ln_gamma, ln_beta))
        q_prime = jax.nn.relu(qh) + EPS_K
        k_prime = (jax.nn.relu(kh) + EPS_K) * em
        vh = vh * em
        kv = jnp.einsum('bhnd,bhne->bhde', k_prime, vh)
        z = 1.0 / (jnp.einsum('bhnd,bhd->bhn', q_prime, k_prime.sum(axis=-2)) + EPS_K)
        att = jnp.einsum('bhnd,bhde,bhn->bhne', q_prime, kv, z)
        att = att.reshape(bsz, -1, D_MODEL)
        out = att @ dense_w + dense_b
        return _layernorm(out, ln_gamma, ln_beta)

    def _L0_ffn_ref(x, gate_w, w1, w2):
        import jax, jax.numpy as jnp
        import numpy as np
        D_MODEL = 256
        NUM_EXPERTS = 8
        TOP_K = 2
        gate_logits = jnp.einsum('bsd,ed->bse', x, gate_w)
        top_v, top_i = jax.lax.top_k(gate_logits, TOP_K)
        gates = jax.nn.softmax(top_v, axis=-1)
        combine = jnp.sum(jax.nn.one_hot(top_i, NUM_EXPERTS, dtype=x.dtype) * gates[..., None], axis=-2)
        out = jnp.zeros_like(x)
        for e in range(NUM_EXPERTS):
            h = jax.nn.relu(jnp.einsum('bsd,fd->bsf', x, w1[e]))
            y = jnp.einsum('bsf,df->bsd', h, w2[e])
            out = out + combine[..., e, None] * y
        return out
    x = x + _L0_xattn_ref(_layernorm(x, axis=-1), ctx_1024, ctx_1024, mask_BxS2_ff1, L0_xattn_wq, L0_xattn_wk, L0_xattn_wv, L0_xattn_ln_gamma, L0_xattn_ln_beta, L0_xattn_dense_w, L0_xattn_dense_b)
    x = x + _L0_ffn_ref(_layernorm(x, axis=-1), L0_ffn_gate_w, L0_ffn_w1, L0_ffn_w2)
    return x

_drawn_inputs = setup_inputs


def setup_inputs(seed=0):
    import zlib

    import numpy as np

    out = dict(_drawn_inputs(seed))
    spreads = {'L0_xattn_ln_gamma': (1.0, 0.2),
     'L0_xattn_ln_beta': (0.0, 0.1),
     'L0_xattn_dense_b': (0.0, 0.1)}
    factors = {}
    for name, (base, spread) in spreads.items():
        noise = np.random.default_rng([zlib.crc32(name.encode()), seed]).standard_normal(out[name].shape)
        drawn = base * np.exp(spread * noise) if base else spread * noise
        out[name] = jnp.asarray(drawn.astype(out[name].dtype))
    for name, factor in factors.items():
        out[name] = (out[name] * factor).astype(out[name].dtype)
    return out
```

```python
from contextlib import ExitStack

import concourse.bass as bass
import numpy as np
from concourse import mybir

F32 = mybir.dt.float32
I32 = mybir.dt.int32
U32 = mybir.dt.uint32
ALU = mybir.AluOpType
ACT = mybir.ActivationFunctionType
AX = mybir.AxisListType

P = 128
B, S, D = 4, 512, 256
N = B * S
DC = D // P
H, DH = 16, 16
HPC = P // DH
E, F, TOPK = 8, 1024, 2
FC = F // P
NT = N // P
NH = S // H
NLT = P // NH
TPB = S // P
ST = N * TOPK // P + E - 1
VA = P + 1
KVW = P + HPC
PAD = N
EPS_IN, EPS_LN, EPS_K = 1e-5, 1e-6, 1e-6

CONSTS = {}
_at = 0
for _name, _width in [("ident", P), ("tri", P), ("ones", P), ("blocks", P), ("heads", HPC), ("iota_p", P),
                      ("iota_st", ST), ("iota_e", E), ("fill", NT), ("restart", E * NT), ("token", NT),
                      ("pad_row", 1), ("eps_in", 1), ("eps_ln", 1)]:
    CONSTS[_name] = (_at, _at + _width)
    _at += _width
CW = _at


def constants():
    c = np.zeros((P, CW), np.float32)
    p = np.arange(P)

    def put(name, value):
        a, b = CONSTS[name]
        c[:, a:b] = value

    put("ident", np.eye(P))
    put("tri", p[:, None] < p[None, :])
    put("ones", 1.0)
    put("blocks", p[:, None] // DH == p[None, :] // DH)
    put("heads", p[:, None] // DH == np.arange(HPC)[None, :])
    put("iota_p", p[None, :])
    put("iota_st", np.arange(ST)[None, :])
    put("iota_e", np.arange(E)[None, :])
    put("fill", P * np.arange(NT)[None, :])
    put("restart", (np.arange(E * NT) % NT != 0)[None, :])
    put("token", p[:, None] + P * np.arange(NT)[None, :])
    put("pad_row", PAD + p[:, None])
    put("eps_in", EPS_IN)
    put("eps_ln", EPS_LN)
    return c


def build(nc, xq, xr, ctxT, maskT, wq, wkv, wd, gamma2, beta2, bd, gw, w1, w2, consts, out):
    x2_rows = nc.dram_tensor("x2_rows", [N + P, D], F32).ap()

    with ExitStack() as stack:
        def sb(name, shape, dt=F32):
            return stack.enter_context(nc.sbuf_tensor(name, shape, dt))

        def sem(name):
            return stack.enter_context(nc.semaphore(name))

        bank = [stack.enter_context(nc.psum_tensor(f"bank{i}", [P, 512], F32)) for i in range(8)]

        w1_sb = sb("w1_sb", [P, E, DC, F])
        w2_sb = sb("w2_sb", [P, E, FC, D])
        wq_sb = sb("wq_sb", [P, DC, D])
        wkv_sb = sb("wkv_sb", [P, DC, 2 * D])
        wd_sb = sb("wd_sb", [P, DC, D])
        gw_sb = sb("gw_sb", [P, DC, E])
        gamma_sb = sb("gamma_sb", [P, 2 * D])
        beta_sb = sb("beta_sb", [P, 2 * D])
        bd_sb = sb("bd_sb", [1, D])
        c_sb = sb("c_sb", [P, CW])

        def const(name):
            a, b = CONSTS[name]
            return c_sb[:, a:b]

        ident = const("ident")

        x_sb = sb("x_sb", [P, NT, D])
        mask_sb = sb("mask_sb", [P, NT])
        mask2_sb = sb("mask2_sb", [P, NT])
        ctx_sb = x_sb[:, 0:TPB, :].rearrange("p t (c n) -> p t c n", c=DC)
        kv_stat = sb("kv_stat", [P, 2, 2, 6])
        kv_mv = sb("kv_mv", [P, 2, 2, 2])
        kv_std = sb("kv_std", [P, 2, 2])
        kv_rs = sb("kv_rs", [P, 2, 2])
        kv_nmr = sb("kv_nmr", [P, 2, 2])
        work1 = sb("work1", [P, 10 * D + 2 * DC * VA])
        kv_n = work1[:, 0:4 * D].rearrange("p (a d) -> p a d", a=2)
        kv_g = work1[:, 4 * D:8 * D].rearrange("p (a d) -> p a d", a=2)
        kp_sb = work1[:, 8 * D:10 * D].rearrange("p (a d) -> p a d", a=2)
        va_sb = work1[:, 10 * D:].rearrange("p (a c n) -> p a c n", a=2, c=DC)
        kvbd = sb("kvbd", [P, B, DC, KVW])

        xq_sb = sb("xq_sb", [P, TPB, D])
        att_sb = w2_sb[:, 4:6].rearrange("p a c d -> p (a c) d").rearrange("p (b g) d -> p b g d", b=B)
        heads_sb = w2_sb[:, 6:8].rearrange("p a c d -> p (a c) d")
        work = sb("work", [P, 11, 2, D])
        xn_sb, xT_sb, qn_sb, qg_sb, qpT_sb, head_sb, aT_sb, on_sb, x1_sb, x2_sb, x2T_sb = (work[:, i] for i in range(11))
        z_sb = sb("z_sb", [P, 2, H])
        stat = {k: sb(f"stat_{k}", [P, 2, 6]) for k in "xqor"}
        mv = {k: sb(f"mv_{k}", [P, 2, 2]) for k in "xqor"}
        std = {k: sb(f"std_{k}", [P, 2, 1]) for k in "xqor"}
        rs = {k: sb(f"rs_{k}", [P, 2, 1]) for k in "xqor"}
        nmr = {k: sb(f"nmr_{k}", [P, 2, 1]) for k in "xqor"}
        lg_sb = sb("lg_sb", [P, 2, E])
        top_v = sb("top_v", [P, 2, 8])
        top_i = sb("top_i", [P, 2, 8], U32)

        carved = [0]

        def carve(*shape):
            size = int(np.prod(shape))
            a = carved[0]
            carved[0] += size
            names = "abc"[:len(shape)]
            spread = " ".join(names)
            return work1[:, a:a + size].rearrange(f"p ({spread}) -> p {spread}", **dict(zip(names, shape)))

        onehot = carve(TOPK * NT, E).rearrange("p (k t) e -> p k t e", k=TOPK)
        choice_v, choice_i = carve(TOPK, NT), carve(TOPK, NT)
        picked = carve(TOPK * NT, E)
        chosen = carve(NT, E)
        totT, incl, tiles_cmp, base = (carve(E, NT) for _ in range(4))
        pos = carve(NT, E)
        exp_cmp = carve(ST, E)
        gdiff = carve(3, NT)
        gate = carve(TOPK, NT)
        tiles_of = carve(E)
        ends = carve(E)
        starts = carve(E)
        dest = carve(TOPK * NT)
        dest_i = carve(TOPK * NT).bitcast(I32)
        tile_i = carve(TOPK * NT).bitcast(I32)
        row_i = carve(TOPK * NT).bitcast(I32)
        tile_f = carve(TOPK * NT)
        row_f = carve(TOPK * NT)
        load_f = carve(TOPK * NT)
        used = work[:, :, :, :].rearrange("p i a d -> p (i a d)")
        pairs = TOPK * NT * ST
        in_tile = used[:, 0:pairs].rearrange("p (k s) -> p k s", s=ST)
        carry = used[:, pairs:3 * pairs].rearrange("p (k a s) -> p k a s", a=2, s=ST)
        in_row = x_sb[:, :, :].rearrange("p t (a r) -> p (t a) r", a=2)
        exp_f = carve(ST)
        exp_i = carve(ST).bitcast(I32)
        slot_f = carve(ST)
        slot_row = carve(ST).bitcast(U32)
        slot_gate = carve(ST)

        h_sb = x_sb[:, 0:4, :].rearrange("p a b -> p (a b)")
        hT_sb = x_sb[:, 4:8, :].rearrange("p a b -> p (a b)")
        xg_sb = x_sb[:, 8:10, :]
        gT_sb = x_sb[:, 10:12, :]
        y_sb = x_sb[:, 12:14, :]
        row_sb = sb("row_sb", [P, 2, 1], U32)
        grow_sb = sb("grow_sb", [P, 2, 1], U32)
        zero_sb = sb("zero_sb", [P, D])

        kv_ps, kvacc_ps = bank[0:4], bank[4:6]
        xT_ps, q_ps, qT_ps, att_ps = bank[6], bank[7], bank[0], bank[1]
        aT_ps, o_ps, x2T_ps, lg_ps = bank[4], bank[5], bank[2], bank[3]
        within_ps, total_ps, slots_ps = bank[6], bank[7], bank[0]
        h_ps, hT_ps, gT_ps, y_ps = bank[0:2], bank[2:4], bank[4], bank[5:7]

        consts_in, wkv_in, ctx_in, x_in = sem("consts_in"), sem("wkv_in"), [sem(f"ctx_in{i}") for i in range(4)], sem("x_in")
        small_in, w_in = sem("small_in"), sem("w_in")
        kv_done, kvstat_1, kvstat_2, kvmv_1, kvmv_2, kvstd_done, kvrs_done, kvnmr_done = (
            sem(n) for n in ("kv_done", "kvstat_1", "kvstat_2", "kvmv_1", "kvmv_2", "kvstd_done", "kvrs_done", "kvnmr_done"))
        kn_done, vn_done, kvgamma_done, kvbeta_done = (sem(n) for n in ("kn_done", "vn_done", "kvgamma_done", "kvbeta_done"))
        kp_done, va_done, vmask_done, acc_done, mask2_done = (sem(n) for n in ("kp_done", "va_done", "vmask_done", "acc_done", "mask2_done"))
        kvbd_done, kvsum_done = sem("kvbd_done"), sem("kvsum_done")
        xq_in = [sem(f"xq_in{i}") for i in range(TPB)]
        spread_in = [sem(f"spread_in{i}") for i in range(B)]
        xn_done, xTps_done, xT_done, q_done, qn_done, qgamma_done, qg_done = (
            sem(n) for n in ("xn_done", "xTps_done", "xT_done", "q_done", "qn_done", "qgamma_done", "qg_done"))
        qTps_done, qpT_done, attps_done, den_done, z_done, att_done = (
            sem(n) for n in ("qTps_done", "qpT_done", "attps_done", "den_done", "z_done", "att_done"))
        head_done = sem("head_done")
        aTps_done, aT_done, o_done, on_done, ogamma_done, og_done = (
            sem(n) for n in ("aTps_done", "aT_done", "o_done", "on_done", "ogamma_done", "og_done"))
        x1_done, x2_done, x2Tps_done, x2T_done, lgps_done = (
            sem(n) for n in ("x1_done", "x2_done", "x2Tps_done", "x2T_done", "lgps_done"))
        x1_stored, x2_stored = ([sem(f"{n}{i}") for i in range(2)] for n in ("x1_stored", "x2_stored"))
        lg_done, topv_done, topi_done, choicev_done, choicei_done = (
            sem(n) for n in ("lg_done", "topv_done", "topi_done", "choicev_done", "choicei_done"))
        stat_done = {k: sem(f"stat_done_{k}") for k in "xqor"}
        mv_done = {k: sem(f"mv_done_{k}") for k in "xqor"}
        std_done = {k: sem(f"std_done_{k}") for k in "xqor"}
        rs_done = {k: sem(f"rs_done_{k}") for k in "xqor"}
        nmr_done = {k: sem(f"nmr_done_{k}") for k in "xqor"}
        slot_step, chosen_done, within_done, total_done, gdiff_done, gexp_done = (
            sem(n) for n in ("slot_step", "chosen_done", "within_done", "total_done", "gdiff_done", "gexp_done"))
        spread_done, slots_done, exp_done, slot_done, gate_done = (
            sem(n) for n in ("spread_done", "slots_done", "exp_done", "slot_done", "gate_done"))
        zero_done, zero_stored = sem("zero_done"), sem("zero_stored")
        gathered = [sem(f"gathered{i}") for i in range(2)]
        grow_done, row_done, gTps_done, gT_done, hps_done, relu_done = (
            sem(n) for n in ("grow_done", "row_done", "gTps_done", "gT_done", "hps_done", "relu_done"))
        grow_first = sem("grow_first")
        hTps_done, hT_done, yps_done, y_done, added = (
            sem(n) for n in ("hTps_done", "hT_done", "yps_done", "y_done", "added"))

        def wait(eng, s, count):
            if not isinstance(count, int) or count > 0:
                eng.wait_ge(s, count)

        def plain(eng, *needs):
            eng.wait_ge(consts_in, 16)
            for s, count in needs:
                wait(eng, s, count)

        def live(t, n):
            return not isinstance(t, int) or 0 <= t < n

        def col(t):
            return bass.DynSlice(t, 1)

        def behind(t, u, k):
            return t - k, (u - k) % TPB

        def batch_of(t, u):
            return t // TPB if isinstance(t, int) else (t - u) // TPB

        def pass1(eng, step):
            for t in range(TPB):
                step(t, t)
            with eng.Fori(1, B) as b:
                for u in range(TPB):
                    step(b * TPB + u, u)
            for t in range(NT, NT + 3):
                step(t, t % TPB)

        def pass2(eng, step):
            for t in range(TPB):
                step(t, t)
            with eng.Fori(1, B) as b:
                for u in range(TPB):
                    step(b * TPB + u, u)
            for t in range(NT, NT + 2):
                step(t, t - NT)

        def pass3(eng, step):
            for t in range(4):
                step(t, t % 2)
            with eng.Fori(2, NT // 2) as i:
                for u in range(2):
                    step(i * 2 + u, u)
            for t in range(NT, NT + 2):
                step(t, t % 2)

        def pass4(eng, step):
            for j in range(2):
                step(j, j)
            with eng.Fori(1, (ST - 3) // 2) as i:
                for u in range(2):
                    step(i * 2 + u, u)
            for j in range((ST - 3) // 2 * 2, ST):
                step(j, j % 2)

        block = stack.enter_context(nc.Block())

        @block.sync
        def _(sp):
            sp.dma_start(c_sb[:, :], consts).then_inc(consts_in, 16)
            sp.dma_start(wkv_sb[:, :, :], wkv).then_inc(wkv_in, 16)
            for u in range(TPB):
                sp.dma_start(ctx_sb[:, u], ctxT[:, u]).then_inc(ctx_in[u], 16)
            for dst, src in ((gamma_sb[:, :], gamma2.partition_broadcast(P)), (beta_sb[:, :], beta2.partition_broadcast(P)),
                             (mask_sb[:, :], maskT), (wq_sb[:, :, :], wq), (wd_sb[:, :, :], wd), (gw_sb[:, :, :], gw),
                             (bd_sb[:, :], bd)):
                sp.dma_start(dst, src).then_inc(small_in, 16)
            for u in range(TPB):
                sp.dma_start(xq_sb[:, u], xq[:, u]).then_inc(xq_in[u], 16)
            with sp.Fori(1, B) as b:
                for u in range(TPB):
                    t = b * TPB + u
                    sp.wait_ge(kv_done, t - (TPB - 1))
                    sp.dma_start(ctx_sb[:, u], ctxT[:, col(t)].rearrange("p a c n -> p (a c) n")).then_inc(ctx_in[u], 16)
            sp.wait_ge(zero_done, 1)
            sp.dma_start(x2_rows[N:N + P, :], zero_sb[:, :]).then_inc(zero_stored, 16)
            sp.dma_start(out[N:N + P, :], zero_sb[:, :]).then_inc(zero_stored, 16)

            sp.wait_ge(kv_done, NT)
            sp.dma_start(x_sb[:, :, :], xr).then_inc(x_in, 16)

            def spread(b):
                sp.wait_ge(att_done, (b + 1) * TPB)
                for i in range(NLT):
                    sp.dma_start(heads_sb[b * NH:(b + 1) * NH, i::NLT, :],
                                 att_sb[i * NH:(i + 1) * NH, b]).then_inc(spread_in[b], 16)

            for b in range(1, B + 1):
                if b < B:
                    for u in range(TPB):
                        sp.wait_ge(xn_done, (b - 1) * TPB + u + 1)
                        sp.dma_start(xq_sb[:, u], xq[:, b * TPB + u]).then_inc(xq_in[u], 16)
                spread(b - 1)
            for b in range(B):
                sp.wait_ge(spread_in[b], 16 * NLT)
            for e in (4, 5):
                sp.dma_start(w2_sb[:, e], w2[:, e]).then_inc(w_in, 16)

            def step(t, u):
                s, us = t - 1, (u - 1) % 2
                if live(s, NT):
                    wait(sp, x1_done, s + 1)
                    sp.dma_start(out[bass.DynSlice(s * P, P), :], x1_sb[:, us]).then_inc(x1_stored[us], 16)
                    wait(sp, x2_done, s + 1)
                    sp.dma_start(x2_rows[bass.DynSlice(s * P, P), :], x2_sb[:, us]).then_inc(x2_stored[us], 16)
            pass3(sp, step)
            sp.wait_ge(head_done, NT)
            for e in (6, 7):
                sp.dma_start(w2_sb[:, e], w2[:, e]).then_inc(w_in, 16)

        @block.tensor
        def _(pe):
            def transpose(dst, src, chunks, done):
                for c in range(chunks):
                    last = nc.tensor.transpose(dst[:, c * P:(c + 1) * P], src[:, c * P:(c + 1) * P], ident)
                last.then_inc(done, 1)

            pe.wait_ge(consts_in, 16)
            pe.wait_ge(wkv_in, 16)

            def step1(t, u):
                if live(t, NT):
                    wait(pe, ctx_in[u], 16 * ((t - u) // TPB + 1) if isinstance(t, int) else (t - u) * (16 // TPB) + 16)
                    wait(pe, vn_done, t - (TPB - 1))
                    for c in range(DC):
                        last = nc.tensor.matmul(kv_ps[u][:, :], ctx_sb[:, u, c, :], wkv_sb[:, c, :],
                                                start=(c == 0), stop=(c == DC - 1))
                    last.then_inc(kv_done, 1)
                s, us = t - 3, (u - 3) % TPB
                if live(s, NT):
                    wait(pe, va_done, s + 1)
                    wait(pe, vmask_done, s + 1)
                    wait(pe, kp_done, s + 1)
                    if us == 0:
                        if isinstance(s, int):
                            wait(pe, kvsum_done, s // TPB * DC)
                        else:
                            wait(pe, kvsum_done, (s - us) // TPB * DC)
                    for c in range(DC):
                        last = nc.tensor.matmul(kvacc_ps[c][:, 0:VA], kp_sb[:, us % 2, c * P:(c + 1) * P],
                                                va_sb[:, us % 2, c, :], start=(us == 0), stop=(us == TPB - 1))
                    last.then_inc(acc_done, 1)
            pass1(pe, step1)

            pe.wait_ge(small_in, 16 * 7)

            def step2(t, u):
                s, us = behind(t, u, 2)
                t, u = behind(t, u, 1)
                par = u % 2
                if live(t, NT):
                    wait(pe, xn_done, t + 1)
                    wait(pe, xT_done, t)
                    transpose(xT_ps, xn_sb[:, par], DC, xTps_done)
                if live(s, NT):
                    if isinstance(s, int) and s == 0:
                        pe.wait_ge(vn_done, NT)
                    wait(pe, qg_done, s + 1)
                    wait(pe, qpT_done, s)
                    transpose(qT_ps, qg_sb[:, us % 2], DC, qTps_done)
                if live(t, NT):
                    wait(pe, xT_done, t + 1)
                    wait(pe, qn_done, t)
                    for c in range(DC):
                        last = nc.tensor.matmul(q_ps[:, 0:D], xT_sb[:, par, c * P:(c + 1) * P], wq_sb[:, c, :],
                                                start=(c == 0), stop=(c == DC - 1))
                    last.then_inc(q_done, 1)
                if live(s, NT):
                    b = batch_of(s, us)
                    wait(pe, kvbd_done, (b + 1) * DC)
                    wait(pe, kvsum_done, (b + 1) * DC)
                    wait(pe, qpT_done, s + 1)
                    wait(pe, att_done, s)
                    batch = kvbd[:, col(b)].rearrange("p a c n -> p (a c) n")
                    for c in range(DC):
                        last = nc.tensor.matmul(att_ps[:, c * KVW:(c + 1) * KVW], qpT_sb[:, us % 2, c * P:(c + 1) * P],
                                                batch[:, c, :], start=True, stop=True)
                    last.then_inc(attps_done, 1)
            pass2(pe, step2)

            pe.wait_ge(kvsum_done, DC * B)

            def step3(t, u):
                if live(t, NT):
                    wait(pe, head_done, t + 1)
                    wait(pe, aT_done, t)
                    transpose(aT_ps, head_sb[:, u], DC, aTps_done)
                s, us = t - 2, u
                if live(s, NT):
                    wait(pe, x2_done, s + 1)
                    wait(pe, x2T_done, s)
                    transpose(x2T_ps, x2_sb[:, us], DC, x2Tps_done)
                if live(t, NT):
                    wait(pe, aT_done, t + 1)
                    wait(pe, on_done, t)
                    for c in range(DC):
                        nc.tensor.matmul(o_ps[:, 0:D], aT_sb[:, u, c * P:(c + 1) * P], wd_sb[:, c, :],
                                         start=(c == 0), stop=False)
                    nc.tensor.matmul(o_ps[:, 0:D], const("ones")[0:1, :], bd_sb[0:1, :],
                                     start=False, stop=True).then_inc(o_done, 1)
                if live(s, NT):
                    wait(pe, x2T_done, s + 1)
                    wait(pe, lg_done, s)
                    for c in range(DC):
                        last = nc.tensor.matmul(lg_ps[:, 0:E], x2T_sb[:, us, c * P:(c + 1) * P], gw_sb[:, c, :],
                                                start=(c == 0), stop=(c == DC - 1))
                    last.then_inc(lgps_done, 1)
            pass3(pe, step3)

            pe.wait_ge(chosen_done, 1)
            flat = chosen[:, :, :].rearrange("p t e -> p (t e)")
            nc.tensor.matmul(within_ps[:, 0:NT * E], const("tri"), flat, start=True, stop=True).then_inc(within_done, 1)
            nc.tensor.matmul(total_ps[:, 0:NT * E], const("ones"), flat, start=True, stop=True).then_inc(total_done, 1)
            for k in range(TOPK * NT):
                if k % NT == 0:
                    pe.wait_ge(spread_done, k // NT + 1)
                last = nc.tensor.matmul(slots_ps[:, 0:2 * ST], in_row[:, k, :], carry[:, k].rearrange("p a s -> p (a s)"),
                                        start=(k == 0), stop=(k == TOPK * NT - 1))
            last.then_inc(slots_done, 1)

            pe.wait_ge(exp_done, 1)
            pe.wait_ge(slot_done, 1)
            pe.wait_ge(w_in, 16 * 2 * E)

            def rows_T(j, par):
                wait(pe, gathered[par], (j - par) * 8 + 16)
                wait(pe, gT_done, j)
                transpose(gT_ps, xg_sb[:, par], DC, gTps_done)

            def layer1(j, par):
                e = pe.value_load(exp_i[0:1, col(j)], min_val=0, max_val=E - 1)
                w = w1_sb[:, col(e)].rearrange("p a c f -> p (a c) f")
                wait(pe, gT_done, j + 1)
                for half in range(2):
                    wait(pe, relu_done, (j - 1) * 2 + half + 1)
                    for c in range(DC):
                        last = nc.tensor.matmul(h_ps[half][:, :], gT_sb[:, par, c * P:(c + 1) * P],
                                                w[:, c, half * 512:(half + 1) * 512], start=(c == 0), stop=(c == DC - 1))
                    last.then_inc(hps_done, 1)

            def step4(j, par):
                for half in range(2):
                    wait(pe, relu_done, j * 2 + half + 1)
                    if live(j - 1, ST):
                        wait(pe, hT_done, (j - 1) * 2 + half + 1)
                    transpose(hT_ps[half], h_sb[:, half * 512:(half + 1) * 512], 4, hTps_done)
                if live(j + 1, ST):
                    layer1(j + 1, 1 - par)
                if live(j + 2, ST):
                    rows_T(j + 2, par)
                e = pe.value_load(exp_i[0:1, col(j)], min_val=0, max_val=E - 1)
                w = w2_sb[:, col(e)].rearrange("p a c d -> p (a c) d")
                wait(pe, y_done, j - 1)
                for c in range(FC):
                    if c % 4 == 0:
                        wait(pe, hT_done, j * 2 + c // 4 + 1)
                    last = nc.tensor.matmul(y_ps[par][:, 0:D], hT_sb[:, c * P:(c + 1) * P], w[:, c, :],
                                            start=(c == 0), stop=(c == FC - 1))
                last.then_inc(yps_done, 1)
            rows_T(0, 0)
            rows_T(1, 1)
            layer1(0, 0)
            pass4(pe, step4)

        @block.scalar
        def _(act):
            def norm(dst, src, r, m, done):
                nc.scalar.activation(dst, src, ACT.Identity, bias=m, scale=r).then_inc(done, 1)

            def root(k, s, us, eps):
                wait(act, mv_done[k], s + 1)
                wait(act, rs_done[k], s - 1)
                nc.scalar.activation(std[k][:, us], mv[k][:, us, 1:2], ACT.Sqrt, bias=const(eps)).then_inc(std_done[k], 1)

            act.wait_ge(consts_in, 16)

            def weights(e):
                act.dma_start(w1_sb[:, e], w1[:, e]).then_inc(w_in, 16)
                if e < 4:
                    act.dma_start(w2_sb[:, e], w2[:, e]).then_inc(w_in, 16)

            def step1(t, u):
                par = u % 2
                if live(t, NT):
                    wait(act, kvmv_1, t + 1)
                    wait(act, kvmv_2, t + 1)
                    wait(act, kvrs_done, t - 1)
                    nc.scalar.activation(kv_std[:, par], kv_mv[:, par, :, 1], ACT.Sqrt,
                                         bias=const("eps_ln")).then_inc(kvstd_done, 1)
                s, us = t - 1, (u - 1) % TPB
                par = us % 2
                if live(s, NT):
                    wait(act, kvnmr_done, s + 1)
                    wait(act, kvgamma_done, s - 1)
                    norm(kv_n[:, par, 0:D], kv_ps[us][:, 0:D], kv_rs[:, par, 0:1], kv_nmr[:, par, 0:1], kn_done)
                    norm(kv_n[:, par, D:], kv_ps[us][:, D:], kv_rs[:, par, 1:2], kv_nmr[:, par, 1:2], vn_done)
                if isinstance(t, int) and t < 4:
                    weights(t)
            pass1(act, step1)
            for e in range(4, E):
                weights(e)

            def step2(t, u):
                if live(t, NT):
                    root("x", t, u % 2, "eps_in")
                t, u = behind(t, u, 1)
                par = u % 2
                if live(t, NT):
                    wait(act, xTps_done, t + 1)
                    wait(act, q_done, t - 1)
                    nc.scalar.copy(xT_sb[:, par], xT_ps[:, 0:D]).then_inc(xT_done, 1)
                    root("q", t, par, "eps_ln")
                    wait(act, nmr_done["q"], t + 1)
                    wait(act, qgamma_done, t - 1)
                    norm(qn_sb[:, par], q_ps[:, 0:D], rs["q"][:, par], nmr["q"][:, par], qn_done)
            pass2(act, step2)

            def step3(t, u):
                if live(t, NT):
                    wait(act, aTps_done, t + 1)
                    wait(act, o_done, t - 1)
                    nc.scalar.copy(aT_sb[:, u], aT_ps[:, 0:D]).then_inc(aT_done, 1)
                s, us = t - 2, u
                if live(s, NT):
                    wait(act, x2Tps_done, s + 1)
                    wait(act, lgps_done, s - 1)
                    nc.scalar.copy(x2T_sb[:, us], x2T_ps[:, 0:D]).then_inc(x2T_done, 1)
                s, us = t - 1, (u - 1) % 2
                if live(s, NT):
                    root("r", s, us, "eps_in")
                if live(t, NT):
                    root("o", t, u, "eps_ln")
                    wait(act, nmr_done["o"], t + 1)
                    wait(act, x1_done, t - 1)
                    norm(on_sb[:, u], o_ps[:, 0:D], rs["o"][:, u], nmr["o"][:, u], on_done)
            pass3(act, step3)

            act.wait_ge(gdiff_done, 1)
            nc.scalar.activation(gdiff[:, 1], gdiff[:, 0], ACT.Exp).then_inc(gexp_done, 1)
            act.wait_ge(slots_done, 1)
            act.wait_ge(gate_done, 1)

            def step4(j, par):
                for half in range(2):
                    wait(act, hps_done, j * 2 + half + 1)
                    if live(j - 1, ST):
                        wait(act, hTps_done, (j - 1) * 2 + half + 1)
                    nc.scalar.activation(h_sb[:, half * 512:(half + 1) * 512], h_ps[half][:, :], ACT.Relu).then_inc(relu_done, 1)
                if live(j - 1, ST):
                    gated(j - 1, 1 - par)

            def gated(j, par):
                wait(act, yps_done, j + 1)
                wait(act, added, (j - 1) * 16)
                nc.scalar.mul(y_sb[:, par], y_ps[par][:, 0:D], slot_gate[:, col(j)]).then_inc(y_done, 1)
            pass4(act, step4)
            gated(ST - 1, (ST - 1) % 2)

        @block.gpsimd
        def _(pool):
            nc.gpsimd.memset(zero_sb[:, :], 0.0).then_inc(zero_done, 1)
            pool.wait_ge(small_in, 16 * 7)

            def step1(t, u):
                s, us = t - 1, (u - 1) % 2
                if live(s, NT):
                    wait(pool, kn_done, s + 1)
                    wait(pool, vn_done, s + 1)
                    wait(pool, va_done, s - 1)
                    wait(pool, kp_done, s - 1)
                    nc.gpsimd.tensor_tensor(kv_g[:, us], kv_n[:, us], gamma_sb[:, :], ALU.mult).then_inc(kvgamma_done, 1)
                    wait(pool, kvgamma_done, s + 1)
                    nc.gpsimd.tensor_tensor(kv_g[:, us], kv_g[:, us], beta_sb[:, :], ALU.add).then_inc(kvbeta_done, 1)
            pass1(pool, step1)

            def step2(t, u):
                t, u = behind(t, u, 1)
                par = u % 2
                if live(t, NT):
                    wait(pool, qn_done, t + 1)
                    wait(pool, qTps_done, t - 1)
                    nc.gpsimd.tensor_tensor(qg_sb[:, par], qn_sb[:, par], gamma_sb[:, 0:D], ALU.mult).then_inc(qgamma_done, 1)
                    wait(pool, qgamma_done, t + 1)
                    nc.gpsimd.tensor_tensor(qg_sb[:, par], qg_sb[:, par], beta_sb[:, 0:D], ALU.add).then_inc(qg_done, 1)
            pass2(pool, step2)
            for b in range(B):
                pool.wait_ge(spread_in[b], 16 * NLT)

            def step3(t, u):
                if live(t, NT):
                    wait(pool, aTps_done, t - 1)
                    nc.gpsimd.tensor_copy(head_sb[:, u].rearrange("p (n e) -> p n e", e=DH),
                                          heads_sb[:, :, bass.DynSlice(t * DH, DH)]).then_inc(head_done, 1)
                s, us = t - 1, (u - 1) % 2
                if live(s, NT):
                    wait(pool, on_done, s + 1)
                    nc.gpsimd.tensor_tensor(on_sb[:, us], on_sb[:, us], gamma_sb[:, 0:D], ALU.mult).then_inc(ogamma_done, 1)
                    wait(pool, ogamma_done, s + 1)
                    nc.gpsimd.tensor_tensor(on_sb[:, us], on_sb[:, us], beta_sb[:, 0:D], ALU.add).then_inc(og_done, 1)
            pass3(pool, step3)

            pool.wait_ge(slot_done, 1)
            pool.wait_ge(gate_done, 1)
            for par in range(2):
                pool.wait_ge(x2_stored[par], 16 * NT // 2)
                pool.wait_ge(x1_stored[par], 16 * NT // 2)
            pool.wait_ge(zero_stored, 32)

            def gather(j, par, copied, before):
                nc.gpsimd.tensor_copy(grow_sb[:, par], slot_row[:, col(j)]).then_inc(copied, 1)
                plain(pool, (copied, before))
                nc.gpsimd.indirect_dma_start(
                    out=xg_sb[:, par], out_offset=None, in_=x2_rows,
                    in_offset=bass.IndirectOffsetOnAxis(ap=grow_sb[:, par], axis=0)).then_inc(gathered[par], 16)

            def step4(j, par):
                if live(j + 2, ST):
                    wait(pool, gTps_done, j + 1)
                    wait(pool, gathered[par], (j - par) * 8 + 16)
                    gather(j + 2, par, grow_done, j + 1)
                wait(pool, added, j * 16)
                nc.gpsimd.tensor_copy(row_sb[:, par], slot_row[:, col(j)]).then_inc(row_done, 1)
                plain(pool, (row_done, j + 1), (y_done, j + 1))
                nc.gpsimd.indirect_dma_start(
                    out=out, out_offset=bass.IndirectOffsetOnAxis(ap=row_sb[:, par], axis=0),
                    in_=y_sb[:, par], in_offset=None, compute_op=ALU.add).then_inc(added, 16)
            gather(0, 0, grow_first, 1)
            gather(1, 1, grow_first, 2)
            pass4(pool, step4)
            pool.wait_ge(added, ST * 16)

        @block.vector
        def _(dve):
            def stats(k, s, us, src):
                wait(dve, mv_done[k], s - 1)
                nc.vector.bn_stats(stat[k][:, us], src).then_inc(stat_done[k], 1)
                plain(dve, (stat_done[k], s + 1), (std_done[k], s - 1), (nmr_done[k], s - 1))
                nc.vector.bn_aggr(mv[k][:, us], stat[k][:, us]).then_inc(mv_done[k], 1)

            def scales(k, s, us, used):
                wait(dve, std_done[k], s + 1)
                wait(dve, used, s - 1)
                nc.vector.reciprocal(rs[k][:, us], std[k][:, us]).then_inc(rs_done[k], 1)
                wait(dve, rs_done[k], s + 1)
                nc.vector.scalar_tensor_tensor(nmr[k][:, us], mv[k][:, us, 0:1], -1.0, rs[k][:, us],
                                               ALU.mult, ALU.mult).then_inc(nmr_done[k], 1)

            dve.wait_ge(consts_in, 16)
            dve.wait_ge(small_in, 16 * 7)
            nc.vector.tensor_tensor(mask2_sb[:, :], mask_sb[:, :], mask_sb[:, :], ALU.mult).then_inc(mask2_done, 1)
            dve.wait_ge(mask2_done, 1)

            def step1(t, u):
                par = u % 2
                if live(t, NT):
                    wait(dve, kv_done, t + 1)
                    wait(dve, kvmv_1, t - 1)
                    wait(dve, kvmv_2, t - 1)
                    nc.vector.bn_stats(kv_stat[:, par, 0], kv_ps[u][:, 0:D]).then_inc(kvstat_1, 1)
                    nc.vector.bn_stats(kv_stat[:, par, 1], kv_ps[u][:, D:]).then_inc(kvstat_2, 1)
                    plain(dve, (kvstat_1, t + 1), (kvnmr_done, t - 1), (kvstd_done, t - 1))
                    nc.vector.bn_aggr(kv_mv[:, par, 0], kv_stat[:, par, 0]).then_inc(kvmv_1, 1)
                    plain(dve, (kvstat_2, t + 1))
                    nc.vector.bn_aggr(kv_mv[:, par, 1], kv_stat[:, par, 1]).then_inc(kvmv_2, 1)
                s, us = t - 1, (u - 1) % 2
                if live(s, NT):
                    wait(dve, kvstd_done, s + 1)
                    wait(dve, vn_done, s - 1)
                    nc.vector.reciprocal(kv_rs[:, us], kv_std[:, us]).then_inc(kvrs_done, 1)
                    wait(dve, kvrs_done, s + 1)
                    nc.vector.scalar_tensor_tensor(kv_nmr[:, us], kv_mv[:, us, :, 0], -1.0, kv_rs[:, us],
                                                   ALU.mult, ALU.mult).then_inc(kvnmr_done, 1)
                s, us = t - 2, u % 2
                if live(s, NT):
                    wait(dve, kvbeta_done, s + 1)
                    wait(dve, acc_done, s - 1)
                    nc.vector.tensor_scalar(kp_sb[:, us], kv_g[:, us, 0:D], 0.0, EPS_K, ALU.max, ALU.add).then_inc(kp_done, 1)
                    nc.vector.tensor_scalar(va_sb[:, us, :, 0:P], kv_g[:, us, D:].rearrange("p (c n) -> p c n", c=DC),
                                            mask2_sb[:, col(s)], None, ALU.mult).then_inc(va_done, 1)
                    nc.vector.tensor_copy(va_sb[:, us, :, P:VA], mask_sb[:, col(s)].unsqueeze(1).to_broadcast([P, DC, 1])).then_inc(vmask_done, 1)
                s, us = t - 3, (u - 3) % TPB
                if live(s, NT) and us == TPB - 1:
                    wait(dve, acc_done, s + 1)
                    batch = kvbd[:, col(s // TPB)].rearrange("p a c n -> p (a c) n")
                    for c in range(DC):
                        nc.vector.tensor_tensor(batch[:, c, 0:P], kvacc_ps[c][:, 0:P], const("blocks"), ALU.mult).then_inc(kvbd_done, 1)
                        nc.vector.tensor_scalar(batch[:, c, P:KVW], const("heads"), kvacc_ps[c][:, P:VA], None,
                                                ALU.mult).then_inc(kvsum_done, 1)
            pass1(dve, step1)

            def x_stats(t, u):
                wait(dve, xq_in[u], (t + 1) * (16 // TPB) + (TPB - 1 - u) * (16 // TPB))
                stats("x", t, u % 2, xq_sb[:, u])

            def step2(t, u):
                if live(t, NT):
                    x_stats(t, u)
                s, us = behind(t, u, 2)
                if live(s, NT):
                    wait(dve, qTps_done, s + 1)
                    wait(dve, attps_done, s - 1)
                    nc.vector.tensor_scalar(qpT_sb[:, us % 2], qT_ps[:, 0:D], 0.0, EPS_K, ALU.max, ALU.add).then_inc(qpT_done, 1)
                if live(t, NT):
                    scales("x", t, u % 2, xn_done)
                    wait(dve, xTps_done, t - 1)
                    nc.vector.tensor_scalar(xn_sb[:, u % 2], xq_sb[:, u], mv["x"][:, u % 2, 0:1], rs["x"][:, u % 2],
                                            ALU.subtract, ALU.mult).then_inc(xn_done, 1)
                r, ur = behind(t, u, 1)
                if live(r, NT):
                    wait(dve, q_done, r + 1)
                    stats("q", r, ur % 2, q_ps[:, 0:D])
                    scales("q", r, ur % 2, qn_done)
                if live(s, NT):
                    wait(dve, attps_done, s + 1)
                    wait(dve, z_done, s - 1)
                    both = att_ps[:, 0:DC * KVW].rearrange("p (c n) -> p c n", c=DC)
                    z = z_sb[:, us % 2].rearrange("p (c h) -> p c h", c=DC)
                    nc.vector.tensor_scalar(z, both[:, :, P:KVW], EPS_K, None, ALU.add).then_inc(den_done, 1)
                    wait(dve, den_done, s + 1)
                    nc.vector.reciprocal(z_sb[:, us % 2], z_sb[:, us % 2]).then_inc(z_done, 1)
                    wait(dve, z_done, s + 1)
                    rows = att_sb[:, col(batch_of(s, us)), us].rearrange("p a d -> p (a d)")
                    for c in range(DC):
                        last = nc.vector.tensor_tensor(
                            rows[:, c * P:(c + 1) * P].rearrange("p (h e) -> p h e", h=HPC),
                            both[:, c, 0:P].rearrange("p (h e) -> p h e", h=HPC),
                            z[:, c, :].unsqueeze(2).to_broadcast([P, HPC, DH]), ALU.mult)
                    last.then_inc(att_done, 1)
            pass2(dve, step2)
            dve.wait_ge(x_in, 16)

            def step3(t, u):
                s, us = t - 1, (u - 1) % 2
                if live(s, NT):
                    wait(dve, og_done, s + 1)
                    wait(dve, x1_stored[us], (s - us) * 8)
                    wait(dve, x2_done, s - 1)
                    nc.vector.tensor_tensor(x1_sb[:, us], on_sb[:, us], x_sb[:, col(s)].rearrange("p a d -> p (a d)"),
                                            ALU.add).then_inc(x1_done, 1)
                    wait(dve, x1_done, s + 1)
                    stats("r", s, us, x1_sb[:, us])
                if live(t, NT):
                    wait(dve, o_done, t + 1)
                    stats("o", t, u, o_ps[:, 0:D])
                if live(s, NT):
                    scales("r", s, us, x2_done)
                    wait(dve, x2_stored[us], (s - us) * 8)
                    wait(dve, x2Tps_done, s - 1)
                    nc.vector.tensor_scalar(x2_sb[:, us], x1_sb[:, us], mv["r"][:, us, 0:1], rs["r"][:, us],
                                            ALU.subtract, ALU.mult).then_inc(x2_done, 1)
                if live(t, NT):
                    scales("o", t, u, on_done)
                s, us = t - 2, u
                if live(s, NT):
                    wait(dve, lgps_done, s + 1)
                    wait(dve, topi_done, s - 1)
                    nc.vector.tensor_copy(lg_sb[:, us], lg_ps[:, 0:E]).then_inc(lg_done, 1)
                    plain(dve, (lg_done, s + 1), (choicev_done, s - 1))
                    nc.vector.max(top_v[:, us], lg_sb[:, us]).then_inc(topv_done, 1)
                    plain(dve, (topv_done, s + 1), (choicei_done, s - 1))
                    nc.vector.max_index(top_i[:, us], top_v[:, us], lg_sb[:, us]).then_inc(topi_done, 1)
                    nc.vector.tensor_copy(choice_v[:, :, col(s)].rearrange("p k a -> p (k a)"), top_v[:, us, 0:TOPK]).then_inc(choicev_done, 1)
                    wait(dve, topi_done, s + 1)
                    nc.vector.tensor_copy(choice_i[:, :, col(s)].rearrange("p k a -> p (k a)"), top_i[:, us, 0:TOPK]).then_inc(choicei_done, 1)
            pass3(dve, step3)

            steps = [0]

            def chain(ins):
                steps[0] += 1
                ins.then_inc(slot_step, 1)
                dve.wait_ge(slot_step, steps[0])

            tt, ts = nc.vector.tensor_tensor, nc.vector.tensor_scalar
            dve.wait_ge(choicev_done, NT)
            dve.wait_ge(choicei_done, NT)
            experts = const("iota_e").unsqueeze(1)
            for k in range(TOPK):
                chain(tt(onehot[:, k], choice_i[:, k].unsqueeze(2).to_broadcast([P, NT, E]),
                         experts.to_broadcast([P, NT, E]), ALU.is_equal))
            tt(chosen[:, :, :], onehot[:, 0], onehot[:, 1], ALU.add).then_inc(chosen_done, 1)
            tt(gdiff[:, 0], choice_v[:, 1], choice_v[:, 0], ALU.subtract).then_inc(gdiff_done, 1)
            dve.wait_ge(total_done, 1)
            chain(nc.vector.tensor_copy(totT[:, :, :], total_ps[:, 0:NT * E].rearrange("p (t e) -> p e t", e=E)))
            chain(nc.vector.tensor_tensor_scan(incl[:, :, :].rearrange("p e t -> p (e t)"), const("restart"),
                                               totT[:, :, :].rearrange("p e t -> p (e t)"), 0.0, ALU.mult, ALU.add))
            chain(tt(tiles_cmp[:, :, :], incl[:, :, NT - 1:NT].to_broadcast([P, E, NT]),
                     const("fill").unsqueeze(1).to_broadcast([P, E, NT]), ALU.is_gt))
            chain(nc.vector.tensor_reduce(tiles_of[:, :], tiles_cmp[:, :, :], AX.X, ALU.add))
            chain(nc.vector.tensor_tensor_scan(ends[:, :], const("ones")[:, 0:E], tiles_of[:, :], 0.0, ALU.mult, ALU.add))
            chain(tt(starts[:, :], ends[:, :], tiles_of[:, :], ALU.subtract))
            chain(tt(base[:, :, :], incl[:, :, :], totT[:, :, :], ALU.subtract))
            chain(nc.vector.scalar_tensor_tensor(base[:, :, :], starts[:, :].unsqueeze(2).to_broadcast([P, E, NT]), float(P),
                                                 base[:, :, :], ALU.mult, ALU.add))
            dve.wait_ge(within_done, 1)
            chain(tt(pos[:, :, :], within_ps[:, 0:NT * E].rearrange("p (t e) -> p t e", e=E),
                     base[:, :, :].rearrange("p e t -> p t e"), ALU.add))
            for k in range(TOPK):
                chain(tt(picked[:, k * NT:(k + 1) * NT], onehot[:, k], pos[:, :, :], ALU.mult))
            chain(nc.vector.tensor_reduce(dest[:, :], picked[:, :, :], AX.X, ALU.add))
            chain(nc.vector.tensor_copy(dest_i[:, :], dest[:, :]))
            chain(ts(tile_i[:, :], dest_i[:, :], P.bit_length() - 1, None, ALU.logical_shift_right))
            chain(ts(row_i[:, :], dest_i[:, :], P - 1, None, ALU.bitwise_and))
            chain(nc.vector.tensor_copy(tile_f[:, :], tile_i[:, :]))
            chain(nc.vector.tensor_copy(row_f[:, :], row_i[:, :]))
            dve.wait_ge(gexp_done, 1)
            chain(ts(gdiff[:, 2], gdiff[:, 1], 1.0, None, ALU.add))
            chain(nc.vector.reciprocal(gate[:, 0], gdiff[:, 2]))
            chain(tt(gate[:, 1], gate[:, 0], gdiff[:, 1], ALU.mult))
            for k in range(TOPK):
                chain(nc.vector.scalar_tensor_tensor(load_f[:, k * NT:(k + 1) * NT], const("token"), -float(PAD),
                                                     row_f[:, k * NT:(k + 1) * NT], ALU.add, ALU.subtract))
            for k in range(TOPK):
                a, b = k * NT, (k + 1) * NT
                chain(tt(in_row[:, a:b, :], row_f[:, a:b].unsqueeze(2).to_broadcast([P, NT, P]),
                         const("iota_p").unsqueeze(1).to_broadcast([P, NT, P]), ALU.is_equal))
                chain(tt(in_tile[:, a:b, :], tile_f[:, a:b].unsqueeze(2).to_broadcast([P, NT, ST]),
                         const("iota_st").unsqueeze(1).to_broadcast([P, NT, ST]), ALU.is_equal))
                chain(tt(carry[:, a:b, 0, :], in_tile[:, a:b, :], load_f[:, a:b].unsqueeze(2).to_broadcast([P, NT, ST]), ALU.mult))
                tt(carry[:, a:b, 1, :], in_tile[:, a:b, :], gate[:, k].unsqueeze(2).to_broadcast([P, NT, ST]),
                   ALU.mult).then_inc(spread_done, 1)
            chain(tt(exp_cmp[:, :, :], ends[:, :].unsqueeze(1).to_broadcast([P, ST, E]),
                     const("iota_st").unsqueeze(2).to_broadcast([P, ST, E]), ALU.is_le))
            chain(nc.vector.tensor_reduce(exp_f[:, :], exp_cmp[:, :, :], AX.X, ALU.add))
            ts(exp_i[:, :], exp_f[:, :], float(E - 1), None, ALU.min).then_inc(exp_done, 1)
            dve.wait_ge(slots_done, 1)
            chain(ts(slot_f[:, :], slots_ps[:, 0:ST], const("pad_row"), None, ALU.add))
            nc.vector.tensor_copy(slot_row[:, :], slot_f[:, :]).then_inc(slot_done, 1)
            nc.vector.tensor_copy(slot_gate[:, :], slots_ps[:, ST:2 * ST]).then_inc(gate_done, 1)

            def rows_out(j, par):
                wait(dve, gTps_done, j + 1)
                if live(j - 2, ST):
                    wait(dve, hps_done, (j - 2) * 2 + 2)
                nc.vector.tensor_copy(gT_sb[:, par], gT_ps[:, 0:D]).then_inc(gT_done, 1)

            def step4(j, par):
                for half in range(2):
                    wait(dve, hTps_done, j * 2 + half + 1)
                    wait(dve, yps_done, j)
                    nc.vector.tensor_copy(hT_sb[:, half * 512:(half + 1) * 512], hT_ps[half][:, :]).then_inc(hT_done, 1)
                if live(j + 2, ST):
                    rows_out(j + 2, par)
            rows_out(0, 0)
            rows_out(1, 1)
            pass4(dve, step4)


def kernel(x, ctx_1024, mask_BxS2_ff1, L0_xattn_wq, L0_xattn_wk, L0_xattn_wv, L0_xattn_ln_gamma, L0_xattn_ln_beta,
           L0_xattn_dense_w, L0_xattn_dense_b, L0_ffn_gate_w, L0_ffn_w1, L0_ffn_w2):
    import concourse.bacc as bacc
    from concourse.bass_utils import run_bass_kernel_spmd

    def chunked(w):
        return np.asarray(w).reshape(DC, P, -1).transpose(1, 0, 2)

    x = np.asarray(x)
    arrays = {
        "xq": x.reshape(B, NH, TPB, NLT, D).transpose(3, 1, 0, 2, 4).reshape(P, NT, D),
        "xr": x.reshape(B, H, NH, D).transpose(0, 2, 1, 3).reshape(P, NT, D),
        "ctxT": np.asarray(ctx_1024).reshape(NT, P, DC, P).transpose(3, 0, 2, 1),
        "maskT": np.asarray(mask_BxS2_ff1).reshape(NT, P).T,
        "wq": chunked(L0_xattn_wq),
        "wkv": chunked(np.concatenate([L0_xattn_wk, L0_xattn_wv], axis=1)),
        "wd": chunked(L0_xattn_dense_w),
        "gamma2": np.concatenate([L0_xattn_ln_gamma, L0_xattn_ln_gamma]),
        "beta2": np.concatenate([L0_xattn_ln_beta, L0_xattn_ln_beta]),
        "bd": np.asarray(L0_xattn_dense_b).reshape(1, D),
        "gw": chunked(np.asarray(L0_ffn_gate_w).T),
        "w1": np.asarray(L0_ffn_w1).reshape(E, F, DC, P).transpose(3, 0, 2, 1),
        "w2": np.asarray(L0_ffn_w2).reshape(E, D, FC, P).transpose(3, 0, 2, 1),
        "consts": constants(),
    }
    arrays = {f"in_{name}": np.ascontiguousarray(a) for name, a in arrays.items()}
    nc = bacc.Bacc("TRN2", target_bir_lowering=False, num_devices=1)
    args = [nc.dram_tensor(name, a.shape, F32, kind="ExternalInput").ap() for name, a in arrays.items()]
    out = nc.dram_tensor("out", [N + P, D], F32, kind="ExternalOutput").ap()
    build(nc, *args, out)
    result = run_bass_kernel_spmd(nc, [arrays], core_ids=[0])
    rows = result.results[0]["out"][:N].reshape(H, B, NH, D)
    return np.ascontiguousarray(rows.transpose(1, 0, 2, 3)).reshape(B, S, D)
```

```python
from contextlib import ExitStack

import concourse.bass as bass
import numpy as np
from concourse import mybir

F32 = mybir.dt.float32
I32 = mybir.dt.int32
U32 = mybir.dt.uint32
ALU = mybir.AluOpType
ACT = mybir.ActivationFunctionType
AX = mybir.AxisListType

P = 128
B, S, D = 4, 512, 256
N = B * S
DC = D // P
H, DH = 16, 16
HPC = P // DH
E, F, TOPK = 8, 1024, 2
FC = F // P
NT = N // P
NH = S // H
NLT = P // NH
TPB = S // P
ST = N * TOPK // P + E - 1
VA = P + 2
KVW = P + HPC
PAD = N
EPS_IN, EPS_LN, EPS_K = 1e-5, 1e-6, 1e-6

CONSTS = {}
_at = 0
for _name, _width in [("ident", P), ("tri", P), ("ones", P), ("blocks", P), ("heads", HPC), ("iota_p", P),
                      ("iota_st", ST), ("iota_e", E), ("fill", NT), ("restart", E * NT), ("token", NT),
                      ("pad_row", 1), ("eps_in", 1), ("eps_ln", 1)]:
    CONSTS[_name] = (_at, _at + _width)
    _at += _width
CW = _at


def constants():
    c = np.zeros((P, CW), np.float32)
    p = np.arange(P)

    def put(name, value):
        a, b = CONSTS[name]
        c[:, a:b] = value

    put("ident", np.eye(P))
    put("tri", p[:, None] < p[None, :])
    put("ones", 1.0)
    put("blocks", p[:, None] // DH == p[None, :] // DH)
    put("heads", p[:, None] // DH == np.arange(HPC)[None, :])
    put("iota_p", p[None, :])
    put("iota_st", np.arange(ST)[None, :])
    put("iota_e", np.arange(E)[None, :])
    put("fill", P * np.arange(NT)[None, :])
    put("restart", (np.arange(E * NT) % NT != 0)[None, :])
    put("token", p[:, None] + P * np.arange(NT)[None, :])
    put("pad_row", PAD + p[:, None])
    put("eps_in", EPS_IN)
    put("eps_ln", EPS_LN)
    return c


def build(nc, xq, xr, ctxT, maskT, wq, wkv, wd, gamma, beta, gbT, bd, gw, w1, w2, consts, out):
    x2_rows = nc.dram_tensor("x2_rows", [N + P, D], F32).ap()

    with ExitStack() as stack:
        def sb(name, shape, dt=F32):
            return stack.enter_context(nc.sbuf_tensor(name, shape, dt))

        def sem(name):
            return stack.enter_context(nc.semaphore(name))

        bank = [stack.enter_context(nc.psum_tensor(f"bank{i}", [P, 512], F32)) for i in range(8)]

        w1_sb = sb("w1_sb", [P, E, DC, F])
        w2_sb = sb("w2_sb", [P, E, FC, D])
        wq_sb = sb("wq_sb", [P, DC, D])
        wkv_sb = sb("wkv_sb", [P, DC, 2 * D])
        wd_sb = sb("wd_sb", [P, DC, D])
        gw_sb = sb("gw_sb", [P, DC, E])
        gamma_sb = sb("gamma_sb", [P, D])
        beta_sb = sb("beta_sb", [P, D])
        gbT_sb = sb("gbT_sb", [P, 2, DC])
        vgamma_sb = sb("vgamma_sb", [P, DC, P])
        vbeta_sb = sb("vbeta_sb", [P, DC, P])
        bd_sb = sb("bd_sb", [1, D])
        c_sb = sb("c_sb", [P, CW])

        def const(name):
            a, b = CONSTS[name]
            return c_sb[:, a:b]

        ident = const("ident")

        x_sb = sb("x_sb", [P, NT, D])
        mask_sb = sb("mask_sb", [P, NT])
        masks_sb = sb("masks_sb", [P, NT, 2])
        ctx_sb = x_sb[:, 0:TPB, :].rearrange("p t (c n) -> p t c n", c=DC)
        kv_stat = sb("kv_stat", [P, 2, 2, 6])
        kv_mv = sb("kv_mv", [P, 2, 2, 2])
        kv_std = sb("kv_std", [P, 2, 2])
        kv_sc = sb("kv_sc", [P, 2, 2, 2])
        kv_rs, kv_nmr = kv_sc[:, :, 0], kv_sc[:, :, 1]
        v_sc = sb("v_sc", [P, 2, 2])
        work1 = sb("work1", [P, 6 * D + 2 * DC * VA + 160])
        k_n, k_g, kp_sb = (work1[:, i * 2 * D:(i + 1) * 2 * D].rearrange("p (a d) -> p a d", a=2) for i in range(3))
        va_sb = work1[:, 6 * D:6 * D + 2 * DC * VA].rearrange("p (a c n) -> p a c n", a=2, c=DC)
        kvg_sb = sb("kvg_sb", [P, DC, P])
        kvbd = sb("kvbd", [P, B, DC, KVW])

        x_stat = sb("x_stat", [P, 2, 6])
        x_mv1 = sb("x_mv1", [P, 2, 2])
        x_mv = sb("x_mv", [P, NT, 2])
        x_std = sb("x_std", [P, NT])
        x_rs = sb("x_rs", [P, NT])

        xq_sb = w2_sb[:, 2:4].rearrange("p a c d -> p (a c) d")
        att_sb = w2_sb[:, 4:6].rearrange("p a c d -> p (a c) d")
        heads_sb = w2_sb[:, 6:8].rearrange("p a c d -> p (a c) d")
        work = sb("work", [P, 11, 2, D])
        xn_sb, xT_sb, qn_sb, qr_sb, qpT_sb, head_sb, aT_sb, on_sb, x1_sb, x2_sb, x2T_sb = (work[:, i] for i in range(11))
        z_sb = sb("z_sb", [P, 2, H])
        stat = {k: sb(f"stat_{k}", [P, 2, 6]) for k in "qor"}
        mv = {k: sb(f"mv_{k}", [P, 2, 2]) for k in "qor"}
        std = {k: sb(f"std_{k}", [P, 2, 1]) for k in "qor"}
        rs = {k: sb(f"rs_{k}", [P, 2, 1]) for k in "qor"}
        nmr = {k: sb(f"nmr_{k}", [P, 2, 1]) for k in "qor"}
        lg_sb = sb("lg_sb", [P, 2, E])
        top_v = sb("top_v", [P, 2, 8])
        top_i = sb("top_i", [P, 2, 8], U32)

        carved = [0]

        def carve(*shape):
            size = int(np.prod(shape))
            a = carved[0]
            carved[0] += size
            names = "abc"[:len(shape)]
            spread = " ".join(names)
            return work1[:, a:a + size].rearrange(f"p ({spread}) -> p {spread}", **dict(zip(names, shape)))

        onehot = carve(TOPK * NT, E).rearrange("p (k t) e -> p k t e", k=TOPK)
        choice_v, choice_i = carve(TOPK, NT), carve(TOPK, NT)
        picked = carve(TOPK * NT, E)
        chosen = carve(NT, E)
        totT, incl, tiles_cmp, base = (carve(E, NT) for _ in range(4))
        pos = carve(NT, E)
        exp_cmp = carve(ST, E)
        gdiff = carve(3, NT)
        gate = carve(TOPK, NT)
        tiles_of = carve(E)
        ends = carve(E)
        starts = carve(E)
        dest = carve(TOPK * NT)
        dest_i = carve(TOPK * NT).bitcast(I32)
        tile_i = carve(TOPK * NT).bitcast(I32)
        row_i = carve(TOPK * NT).bitcast(I32)
        tile_f = carve(TOPK * NT)
        row_f = carve(TOPK * NT)
        load_f = carve(TOPK * NT)
        used = work[:, :, :, :].rearrange("p i a d -> p (i a d)")
        pairs = TOPK * NT * ST
        in_tile = used[:, 0:pairs].rearrange("p (k s) -> p k s", s=ST)
        carry = used[:, pairs:3 * pairs].rearrange("p (k a s) -> p k a s", a=2, s=ST)
        in_row = x_sb[:, :, :].rearrange("p t (a r) -> p (t a) r", a=2)
        exp_f = carve(ST)
        exp_i = carve(ST).bitcast(I32)
        slot_f = carve(ST)
        slot_row = carve(ST).bitcast(U32)
        slot_gate = carve(ST)

        h_sb = x_sb[:, 0:4, :].rearrange("p a b -> p (a b)")
        hT_sb = x_sb[:, 4:8, :].rearrange("p a b -> p (a b)")
        xg_sb = x_sb[:, 8:10, :]
        gT_sb = x_sb[:, 10:12, :]
        y_sb = x_sb[:, 12:14, :]
        row_sb = sb("row_sb", [P, 2, 1], U32)
        grow_sb = sb("grow_sb", [P, 2, 1], U32)
        zero_sb = sb("zero_sb", [P, D])

        kv_ps, kvacc_ps = bank[0:4], bank[4:6]
        xT_ps, q_ps, qT_ps, att_ps = bank[6], (bank[7], bank[2]), bank[0], bank[1]
        aT_ps, o_ps, x2T_ps, lg_ps = bank[4], (bank[5], bank[1]), bank[2], bank[3]
        within_ps, total_ps, slots_ps = bank[6], bank[7], bank[0]
        h_ps, hT_ps, gT_ps, y_ps = bank[0:2], bank[2:4], bank[4], bank[5:7]

        consts_in, wkv_in, ctx_in, x_in = sem("consts_in"), sem("wkv_in"), [sem(f"ctx_in{i}") for i in range(4)], sem("x_in")
        small_in, w_in = sem("small_in"), sem("w_in")
        kv_done, kvstat_1, kvstat_2, kvmv_1, kvmv_2, kvstd_done, kvrs_done, kvnmr_done = (
            sem(n) for n in ("kv_done", "kvstat_1", "kvstat_2", "kvmv_1", "kvmv_2", "kvstd_done", "kvrs_done", "kvnmr_done"))
        kn_done, vn_done, kvgamma_done, kvbeta_done = (sem(n) for n in ("kn_done", "vn_done", "kvgamma_done", "kvbeta_done"))
        kp_done, va_done, vmask_done, acc_done, mask2_done = (sem(n) for n in ("kp_done", "va_done", "vmask_done", "acc_done", "mask2_done"))
        kvbd_done, kvsum_done, kvg_done, vsc_done, vgb_done = (
            sem(n) for n in ("kvbd_done", "kvsum_done", "kvg_done", "vsc_done", "vgb_done"))
        xb_done = sem("xb_done")
        xq_in, xstat_done, xmv_done, xmvcopy_done, xstd_done, xrs_done = (
            sem(n) for n in ("xq_in", "xstat_done", "xmv_done", "xmvcopy_done", "xstd_done", "xrs_done"))
        spread_in = [sem(f"spread_in{i}") for i in range(B)]
        xn_done, xTps_done, xT_done, q_done, qn_done, relu_q = (
            sem(n) for n in ("xn_done", "xTps_done", "xT_done", "q_done", "qn_done", "relu_q"))
        qTps_done, qpT_done, attps_done, den_done, z_done, att_done = (
            sem(n) for n in ("qTps_done", "qpT_done", "attps_done", "den_done", "z_done", "att_done"))
        head_done = sem("head_done")
        aTps_done, aT_done, o_done, on_done, ogamma_done, og_done = (
            sem(n) for n in ("aTps_done", "aT_done", "o_done", "on_done", "ogamma_done", "og_done"))
        x1_done, x2_done, x2Tps_done, x2T_done, lgps_done = (
            sem(n) for n in ("x1_done", "x2_done", "x2Tps_done", "x2T_done", "lgps_done"))
        x1_stored, x2_stored = ([sem(f"{n}{i}") for i in range(2)] for n in ("x1_stored", "x2_stored"))
        lg_done, topv_done, topi_done, choicev_done, choicei_done = (
            sem(n) for n in ("lg_done", "topv_done", "topi_done", "choicev_done", "choicei_done"))
        stat_done = {k: sem(f"stat_done_{k}") for k in "qor"}
        mv_done = {k: sem(f"mv_done_{k}") for k in "qor"}
        std_done = {k: sem(f"std_done_{k}") for k in "qor"}
        rs_done = {k: sem(f"rs_done_{k}") for k in "qor"}
        nmr_done = {k: sem(f"nmr_done_{k}") for k in "qor"}
        slot_step, chosen_done, within_done, total_done, gdiff_done, gexp_done = (
            sem(n) for n in ("slot_step", "chosen_done", "within_done", "total_done", "gdiff_done", "gexp_done"))
        spread_done, slots_done, exp_done, slot_done, gate_done = (
            sem(n) for n in ("spread_done", "slots_done", "exp_done", "slot_done", "gate_done"))
        zero_done, zero_stored = sem("zero_done"), sem("zero_stored")
        gathered = [sem(f"gathered{i}") for i in range(2)]
        grow_done, row_done, gTps_done, gT_done, hps_done, relu_done = (
            sem(n) for n in ("grow_done", "row_done", "gTps_done", "gT_done", "hps_done", "relu_done"))
        grow_first = sem("grow_first")
        hTps_done, hT_done, yps_done, y_done, added = (
            sem(n) for n in ("hTps_done", "hT_done", "yps_done", "y_done", "added"))

        LAG2, LAG3 = 4, 5
        SMALL = 8

        def wait(eng, s, count):
            if not isinstance(count, int) or count > 0:
                eng.wait_ge(s, count)

        def plain(eng, *needs):
            eng.wait_ge(consts_in, 16)
            for s, count in needs:
                wait(eng, s, count)

        def live(t, n):
            return not isinstance(t, int) or 0 <= t < n

        def col(t):
            return bass.DynSlice(t, 1)

        def behind(t, u, k):
            return t - k, (u - k) % TPB

        def batch_of(t, u):
            return t // TPB if isinstance(t, int) else (t - u) // TPB

        def pass1(eng, step):
            for t in range(TPB):
                step(t, t)
            with eng.Fori(1, B) as b:
                for u in range(TPB):
                    step(b * TPB + u, u)
            for t in range(NT, NT + 3):
                step(t, t % TPB)

        def pass23(eng, step, lag):
            for t in range(8):
                step(t, t % 2)
            with eng.Fori(4, NT // 2) as i:
                for u in range(2):
                    step(i * 2 + u, u)
            for t in range(NT, NT + lag):
                step(t, t % 2)

        def pass4(eng, step):
            for j in range(2):
                step(j, j)
            with eng.Fori(1, (ST - 3) // 2) as i:
                for u in range(2):
                    step(i * 2 + u, u)
            for j in range((ST - 3) // 2 * 2, ST):
                step(j, j % 2)

        block = stack.enter_context(nc.Block())

        @block.sync
        def _(sp):
            sp.dma_start(c_sb[:, :], consts).then_inc(consts_in, 16)
            sp.dma_start(wkv_sb[:, :, :], wkv).then_inc(wkv_in, 16)
            for u in range(TPB):
                sp.dma_start(ctx_sb[:, u], ctxT[:, u]).then_inc(ctx_in[u], 16)
            for dst, src in ((gamma_sb[:, :], gamma.partition_broadcast(P)), (beta_sb[:, :], beta.partition_broadcast(P)),
                             (gbT_sb[:, :, :], gbT),
                             (mask_sb[:, :], maskT), (wq_sb[:, :, :], wq), (wd_sb[:, :, :], wd), (gw_sb[:, :, :], gw),
                             (bd_sb[:, :], bd)):
                sp.dma_start(dst, src).then_inc(small_in, 16)
            sp.dma_start(xq_sb, xq).then_inc(xq_in, 16)
            with sp.Fori(1, B) as b:
                for u in range(TPB):
                    t = b * TPB + u
                    sp.wait_ge(kv_done, t - (TPB - 1))
                    sp.dma_start(ctx_sb[:, u], ctxT[:, col(t)].rearrange("p a c n -> p (a c) n")).then_inc(ctx_in[u], 16)
            sp.wait_ge(zero_done, 1)
            sp.dma_start(x2_rows[N:N + P, :], zero_sb[:, :]).then_inc(zero_stored, 16)
            sp.dma_start(out[N:N + P, :], zero_sb[:, :]).then_inc(zero_stored, 16)

            sp.wait_ge(kv_done, NT)
            sp.dma_start(x_sb[:, :, :], xr).then_inc(x_in, 16)

            def spread(b):
                sp.wait_ge(att_done, (b + 1) * TPB)
                for i in range(NLT):
                    sp.dma_start(heads_sb[b * NH:(b + 1) * NH, i::NLT, :],
                                 att_sb[i * NH:(i + 1) * NH, b * TPB:(b + 1) * TPB]).then_inc(spread_in[b], 16)

            for e in (0, 1):
                sp.dma_start(w2_sb[:, e], w2[:, e]).then_inc(w_in, 16)
            for b in range(B):
                spread(b)
            for b in range(B):
                sp.wait_ge(spread_in[b], 16 * NLT)
            for e in range(2, 6):
                sp.dma_start(w2_sb[:, e], w2[:, e]).then_inc(w_in, 16)

            def step(t, u):
                s, us = t - 3, (u - 3) % 2
                if live(s, NT):
                    wait(sp, x1_done, s + 1)
                    sp.dma_start(out[bass.DynSlice(s * P, P), :], x1_sb[:, us]).then_inc(x1_stored[us], 16)
                s, us = t - 4, u
                if live(s, NT):
                    wait(sp, x2_done, s + 1)
                    sp.dma_start(x2_rows[bass.DynSlice(s * P, P), :], x2_sb[:, us]).then_inc(x2_stored[us], 16)
            pass23(sp, step, LAG3)
            sp.wait_ge(head_done, NT)
            for e in (6, 7):
                sp.dma_start(w2_sb[:, e], w2[:, e]).then_inc(w_in, 16)

        @block.tensor
        def _(pe):
            def transpose(dst, src, chunks, done):
                for c in range(chunks):
                    last = nc.tensor.transpose(dst[:, c * P:(c + 1) * P], src[:, c * P:(c + 1) * P], ident)
                last.then_inc(done, 1)

            pe.wait_ge(consts_in, 16)
            pe.wait_ge(wkv_in, 16)

            def step1(t, u):
                if live(t, NT):
                    wait(pe, ctx_in[u], 16 * ((t - u) // TPB + 1) if isinstance(t, int) else (t - u) * (16 // TPB) + 16)
                    wait(pe, vn_done, t - (TPB - 1))
                    for c in range(DC):
                        last = nc.tensor.matmul(kv_ps[u][:, :], ctx_sb[:, u, c, :], wkv_sb[:, c, :],
                                                start=(c == 0), stop=(c == DC - 1))
                    last.then_inc(kv_done, 1)
                s, us = t - 3, (u - 3) % TPB
                if live(s, NT):
                    wait(pe, vn_done, s + 1)
                    wait(pe, vmask_done, s + 1)
                    wait(pe, kp_done, s + 1)
                    if us == 0:
                        wait(pe, kvbd_done, batch_of(s, us) * DC)
                    for c in range(DC):
                        last = nc.tensor.matmul(kvacc_ps[c][:, 0:VA], kp_sb[:, us % 2, c * P:(c + 1) * P],
                                                va_sb[:, us % 2, c, :], start=(us == 0), stop=(us == TPB - 1))
                    last.then_inc(acc_done, 1)
            pass1(pe, step1)

            pe.wait_ge(small_in, 16 * SMALL)

            def step2(t, u):
                s, us = t - 1, (u - 1) % 2
                if live(s, NT):
                    if isinstance(s, int) and s == 1:
                        pe.wait_ge(vn_done, NT)
                    wait(pe, xT_done, s + 1)
                    wait(pe, qn_done, s - 1)
                    for c in range(DC):
                        last = nc.tensor.matmul(q_ps[us][:, 0:D], xT_sb[:, us, c * P:(c + 1) * P], wq_sb[:, c, :],
                                                start=(c == 0), stop=(c == DC - 1))
                    last.then_inc(q_done, 1)
                if live(t, NT):
                    wait(pe, xn_done, t + 1)
                    wait(pe, xT_done, t)
                    transpose(xT_ps, xn_sb[:, u], DC, xTps_done)
                s, us = t - 2, u
                if live(s, NT):
                    wait(pe, qn_done, s + 1)
                    wait(pe, relu_q, s * DC)
                    transpose(qT_ps, qn_sb[:, us], DC, qTps_done)
                s, us = t - 3, (u - 3) % 2
                if live(s, NT):
                    b = s // TPB
                    wait(pe, kvbd_done, (b + 1) * DC)
                    wait(pe, kvsum_done, (b + 1) * DC)
                    wait(pe, qpT_done, s + 1)
                    wait(pe, att_done, s)
                    batch = kvbd[:, col(b)].rearrange("p a c n -> p (a c) n")
                    for c in range(DC):
                        last = nc.tensor.matmul(att_ps[:, c * KVW:(c + 1) * KVW], qpT_sb[:, us, c * P:(c + 1) * P],
                                                batch[:, c, :], start=True, stop=True)
                    last.then_inc(attps_done, 1)
            pass23(pe, step2, LAG2)

            pe.wait_ge(kvbd_done, DC * B)

            def step3(t, u):
                s, us = t - 1, (u - 1) % 2
                if live(s, NT):
                    wait(pe, aT_done, s + 1)
                    wait(pe, on_done, s - 1)
                    for c in range(DC):
                        nc.tensor.matmul(o_ps[us][:, 0:D], aT_sb[:, us, c * P:(c + 1) * P], wd_sb[:, c, :],
                                         start=(c == 0), stop=False)
                    nc.tensor.matmul(o_ps[us][:, 0:D], const("ones")[0:1, :], bd_sb[0:1, :],
                                     start=False, stop=True).then_inc(o_done, 1)
                if live(t, NT):
                    wait(pe, head_done, t + 1)
                    wait(pe, aT_done, t)
                    transpose(aT_ps, head_sb[:, u], DC, aTps_done)
                s, us = t - 4, u
                if live(s, NT):
                    wait(pe, x2_done, s + 1)
                    wait(pe, x2T_done, s)
                    transpose(x2T_ps, x2_sb[:, us], DC, x2Tps_done)
                s, us = t - 5, (u - 5) % 2
                if live(s, NT):
                    wait(pe, x2T_done, s + 1)
                    wait(pe, lg_done, s)
                    for c in range(DC):
                        last = nc.tensor.matmul(lg_ps[:, 0:E], x2T_sb[:, us, c * P:(c + 1) * P], gw_sb[:, c, :],
                                                start=(c == 0), stop=(c == DC - 1))
                    last.then_inc(lgps_done, 1)
            pass23(pe, step3, LAG3)

            pe.wait_ge(chosen_done, 1)
            flat = chosen[:, :, :].rearrange("p t e -> p (t e)")
            nc.tensor.matmul(within_ps[:, 0:NT * E], const("tri"), flat, start=True, stop=True).then_inc(within_done, 1)
            nc.tensor.matmul(total_ps[:, 0:NT * E], const("ones"), flat, start=True, stop=True).then_inc(total_done, 1)
            for k in range(TOPK * NT):
                if k % NT == 0:
                    pe.wait_ge(spread_done, k // NT + 1)
                last = nc.tensor.matmul(slots_ps[:, 0:2 * ST], in_row[:, k, :], carry[:, k].rearrange("p a s -> p (a s)"),
                                        start=(k == 0), stop=(k == TOPK * NT - 1))
            last.then_inc(slots_done, 1)

            pe.wait_ge(exp_done, 1)
            pe.wait_ge(slot_done, 1)
            pe.wait_ge(w_in, 16 * 2 * E)

            def rows_T(j, par):
                wait(pe, gathered[par], (j - par) * 8 + 16)
                wait(pe, gT_done, j)
                transpose(gT_ps, xg_sb[:, par], DC, gTps_done)

            def layer1(j, par):
                e = pe.value_load(exp_i[0:1, col(j)], min_val=0, max_val=E - 1)
                w = w1_sb[:, col(e)].rearrange("p a c f -> p (a c) f")
                wait(pe, gT_done, j + 1)
                for half in range(2):
                    wait(pe, relu_done, (j - 1) * 2 + half + 1)
                    for c in range(DC):
                        last = nc.tensor.matmul(h_ps[half][:, :], gT_sb[:, par, c * P:(c + 1) * P],
                                                w[:, c, half * 512:(half + 1) * 512], start=(c == 0), stop=(c == DC - 1))
                    last.then_inc(hps_done, 1)

            def step4(j, par):
                for half in range(2):
                    wait(pe, relu_done, j * 2 + half + 1)
                    if live(j - 1, ST):
                        wait(pe, hT_done, (j - 1) * 2 + half + 1)
                    transpose(hT_ps[half], h_sb[:, half * 512:(half + 1) * 512], 4, hTps_done)
                if live(j + 1, ST):
                    layer1(j + 1, 1 - par)
                if live(j + 2, ST):
                    rows_T(j + 2, par)
                e = pe.value_load(exp_i[0:1, col(j)], min_val=0, max_val=E - 1)
                w = w2_sb[:, col(e)].rearrange("p a c d -> p (a c) d")
                wait(pe, y_done, j - 1)
                for c in range(FC):
                    if c % 4 == 0:
                        wait(pe, hT_done, j * 2 + c // 4 + 1)
                    last = nc.tensor.matmul(y_ps[par][:, 0:D], hT_sb[:, c * P:(c + 1) * P], w[:, c, :],
                                            start=(c == 0), stop=(c == FC - 1))
                last.then_inc(yps_done, 1)
            rows_T(0, 0)
            rows_T(1, 1)
            layer1(0, 0)
            pass4(pe, step4)

        @block.scalar
        def _(act):
            def norm(dst, src, r, m, done):
                nc.scalar.activation(dst, src, ACT.Identity, bias=m, scale=r).then_inc(done, 1)

            def root(k, s, us, eps):
                wait(act, mv_done[k], s + 1)
                wait(act, rs_done[k], s - 1)
                nc.scalar.activation(std[k][:, us], mv[k][:, us, 1:2], ACT.Sqrt, bias=const(eps)).then_inc(std_done[k], 1)

            act.wait_ge(consts_in, 16)

            def step1(t, u):
                par = u % 2
                if live(t, NT):
                    wait(act, kvmv_1, t + 1)
                    wait(act, kvmv_2, t + 1)
                    wait(act, kvrs_done, t - 1)
                    nc.scalar.activation(kv_std[:, par], kv_mv[:, par, :, 1], ACT.Sqrt,
                                         bias=const("eps_ln")).then_inc(kvstd_done, 1)
                s, us = t - 1, (u - 1) % TPB
                par = us % 2
                if live(s, NT):
                    wait(act, kvnmr_done, s + 1)
                    wait(act, kvgamma_done, s - 1)
                    norm(k_n[:, par], kv_ps[us][:, 0:D], kv_rs[:, par, 0:1], kv_nmr[:, par, 0:1], kn_done)
                    wait(act, vsc_done, s + 1)
                    wait(act, acc_done, s - 1)
                    norm(va_sb[:, par, :, 0:P], kv_ps[us][:, D:].rearrange("p (c n) -> p c n", c=DC),
                         v_sc[:, par, 0:1], v_sc[:, par, 1:2], vn_done)
                if live(t, NT) and u % 2 == 1:
                    e = (t - u) // 2 + u // 2
                    act.dma_start(w1_sb[:, col(e)].rearrange("p a c f -> p (a c f)"),
                                  w1[:, col(e)].rearrange("p a c f -> p (a c f)")).then_inc(w_in, 16)
            pass1(act, step1)
            act.wait_ge(xmvcopy_done, NT)
            nc.scalar.activation(x_std[:, :], x_mv[:, :, 1], ACT.Sqrt, bias=const("eps_in")).then_inc(xstd_done, 1)

            def step2(t, u):
                s, us = t - 3, (u - 3) % 2
                if live(s, NT):
                    wait(act, qTps_done, s + 1)
                    wait(act, qpT_done, s - 1)
                    for c in range(DC):
                        nc.scalar.activation(qr_sb[:, us, c * P:(c + 1) * P], qT_ps[:, c * P:(c + 1) * P], ACT.Relu,
                                             bias=gbT_sb[:, 1, c:c + 1], scale=gbT_sb[:, 0, c:c + 1]).then_inc(relu_q, 1)
                s, us = t - 2, u
                if live(s, NT):
                    wait(act, nmr_done["q"], s + 1)
                    wait(act, qTps_done, s - 1)
                    norm(qn_sb[:, us], q_ps[us][:, 0:D], rs["q"][:, us], nmr["q"][:, us], qn_done)
                if live(t, NT):
                    wait(act, xTps_done, t + 1)
                    wait(act, q_done, t - 1)
                    nc.scalar.copy(xT_sb[:, u], xT_ps[:, 0:D]).then_inc(xT_done, 1)
                s, us = t - 1, (u - 1) % 2
                if live(s, NT):
                    root("q", s, us, "eps_ln")
            pass23(act, step2, LAG2)

            def step3(t, u):
                s, us = t - 2, u
                if live(s, NT):
                    wait(act, nmr_done["o"], s + 1)
                    wait(act, x1_done, s - 1)
                    norm(on_sb[:, us], o_ps[us][:, 0:D], rs["o"][:, us], nmr["o"][:, us], on_done)
                s, us = t - 3, (u - 3) % 2
                if live(s, NT):
                    root("r", s, us, "eps_in")
                if live(t, NT):
                    wait(act, aTps_done, t + 1)
                    wait(act, o_done, t - 1)
                    nc.scalar.copy(aT_sb[:, u], aT_ps[:, 0:D]).then_inc(aT_done, 1)
                s, us = t - 1, (u - 1) % 2
                if live(s, NT):
                    root("o", s, us, "eps_ln")
                s, us = t - 4, u
                if live(s, NT):
                    wait(act, x2Tps_done, s + 1)
                    wait(act, lgps_done, s - 1)
                    nc.scalar.copy(x2T_sb[:, us], x2T_ps[:, 0:D]).then_inc(x2T_done, 1)
            pass23(act, step3, LAG3)

            act.wait_ge(gdiff_done, 1)
            nc.scalar.activation(gdiff[:, 1], gdiff[:, 0], ACT.Exp).then_inc(gexp_done, 1)
            act.wait_ge(slots_done, 1)
            act.wait_ge(gate_done, 1)

            def step4(j, par):
                for half in range(2):
                    wait(act, hps_done, j * 2 + half + 1)
                    if live(j - 1, ST):
                        wait(act, hTps_done, (j - 1) * 2 + half + 1)
                    nc.scalar.activation(h_sb[:, half * 512:(half + 1) * 512], h_ps[half][:, :], ACT.Relu).then_inc(relu_done, 1)
                if live(j - 1, ST):
                    gated(j - 1, 1 - par)

            def gated(j, par):
                wait(act, yps_done, j + 1)
                wait(act, added, (j - 1) * 16)
                nc.scalar.mul(y_sb[:, par], y_ps[par][:, 0:D], slot_gate[:, col(j)]).then_inc(y_done, 1)
            pass4(act, step4)
            gated(ST - 1, (ST - 1) % 2)

        @block.gpsimd
        def _(pool):
            nc.gpsimd.memset(zero_sb[:, :], 0.0).then_inc(zero_done, 1)
            pool.wait_ge(small_in, 16 * SMALL)

            def step1(t, u):
                s, us = t - 1, (u - 1) % 2
                if live(s, NT):
                    wait(pool, kn_done, s + 1)
                    wait(pool, kp_done, s - 1)
                    nc.gpsimd.tensor_tensor(k_g[:, us], k_n[:, us], gamma_sb[:, :], ALU.mult).then_inc(kvgamma_done, 1)
                    wait(pool, kvgamma_done, s + 1)
                    nc.gpsimd.tensor_tensor(k_g[:, us], k_g[:, us], beta_sb[:, :], ALU.add).then_inc(kvbeta_done, 1)
            pass1(pool, step1)

            pool.wait_ge(x_in, 16)
            with pool.Fori(0, NT) as t:
                nc.gpsimd.tensor_tensor(x_sb[:, col(t)].rearrange("p a d -> p (a d)"), x_sb[:, col(t)].rearrange("p a d -> p (a d)"),
                                        beta_sb[:, :], ALU.add).then_inc(xb_done, 1)
            for b in range(B):
                pool.wait_ge(spread_in[b], 16 * NLT)

            def step3(t, u):
                if live(t, NT):
                    wait(pool, aTps_done, t - 1)
                    nc.gpsimd.tensor_copy(head_sb[:, u].rearrange("p (n e) -> p n e", e=DH),
                                          heads_sb[:, :, bass.DynSlice(t * DH, DH)]).then_inc(head_done, 1)
                s, us = t - 2, u
                if live(s, NT):
                    wait(pool, on_done, s + 1)
                    nc.gpsimd.tensor_tensor(on_sb[:, us], on_sb[:, us], gamma_sb[:, :], ALU.mult).then_inc(og_done, 1)
            pass23(pool, step3, LAG3)

            pool.wait_ge(slot_done, 1)
            pool.wait_ge(gate_done, 1)
            for par in range(2):
                pool.wait_ge(x2_stored[par], 16 * NT // 2)
                pool.wait_ge(x1_stored[par], 16 * NT // 2)
            pool.wait_ge(zero_stored, 32)

            def gather(j, par, copied, before):
                nc.gpsimd.tensor_copy(grow_sb[:, par], slot_row[:, col(j)]).then_inc(copied, 1)
                plain(pool, (copied, before))
                nc.gpsimd.indirect_dma_start(
                    out=xg_sb[:, par], out_offset=None, in_=x2_rows,
                    in_offset=bass.IndirectOffsetOnAxis(ap=grow_sb[:, par], axis=0)).then_inc(gathered[par], 16)

            def step4(j, par):
                if live(j + 3, ST):
                    wait(pool, gathered[1 - par], (j + 1) * 8 + 8 + 8 * par)
                    wait(pool, gTps_done, j + 2)
                    gather(j + 3, 1 - par, grow_done, j + 1)
                wait(pool, added, j * 16)
                nc.gpsimd.tensor_copy(row_sb[:, par], slot_row[:, col(j)]).then_inc(row_done, 1)
                plain(pool, (row_done, j + 1), (y_done, j + 1))
                nc.gpsimd.indirect_dma_start(
                    out=out, out_offset=bass.IndirectOffsetOnAxis(ap=row_sb[:, par], axis=0),
                    in_=y_sb[:, par], in_offset=None, compute_op=ALU.add).then_inc(added, 16)
            gather(0, 0, grow_first, 1)
            gather(1, 1, grow_first, 2)
            pool.wait_ge(gTps_done, 1)
            pool.wait_ge(gathered[0], 16)
            gather(2, 0, grow_first, 3)
            pass4(pool, step4)
            pool.wait_ge(added, ST * 16)

        @block.vector
        def _(dve):
            def stats(k, s, us, src):
                wait(dve, mv_done[k], s - 1)
                nc.vector.bn_stats(stat[k][:, us], src).then_inc(stat_done[k], 1)
                plain(dve, (stat_done[k], s + 1), (std_done[k], s - 1), (nmr_done[k], s - 1))
                nc.vector.bn_aggr(mv[k][:, us], stat[k][:, us]).then_inc(mv_done[k], 1)

            def scales(k, s, us, used):
                wait(dve, std_done[k], s + 1)
                wait(dve, used, s - 1)
                nc.vector.reciprocal(rs[k][:, us], std[k][:, us]).then_inc(rs_done[k], 1)
                wait(dve, rs_done[k], s + 1)
                nc.vector.scalar_tensor_tensor(nmr[k][:, us], mv[k][:, us, 0:1], -1.0, rs[k][:, us],
                                               ALU.mult, ALU.mult).then_inc(nmr_done[k], 1)

            dve.wait_ge(consts_in, 16)
            dve.wait_ge(small_in, 16 * SMALL)
            nc.vector.tensor_copy(masks_sb[:, :, 0], mask_sb[:, :]).then_inc(mask2_done, 1)
            nc.vector.tensor_tensor(masks_sb[:, :, 1], mask_sb[:, :], mask_sb[:, :], ALU.mult).then_inc(mask2_done, 1)
            for c in range(DC):
                for dst, src in ((vgamma_sb, gamma_sb), (vbeta_sb, beta_sb)):
                    nc.vector.tensor_tensor(dst[:, c], src[:, c * P:(c + 1) * P], const("blocks"), ALU.mult).then_inc(vgb_done, 1)
            dve.wait_ge(mask2_done, 2)

            def step1(t, u):
                par = u % 2
                if live(t, NT):
                    wait(dve, kv_done, t + 1)
                    wait(dve, kvmv_1, t - 1)
                    wait(dve, kvmv_2, t - 1)
                    nc.vector.bn_stats(kv_stat[:, par, 0], kv_ps[u][:, 0:D]).then_inc(kvstat_1, 1)
                    nc.vector.bn_stats(kv_stat[:, par, 1], kv_ps[u][:, D:]).then_inc(kvstat_2, 1)
                    plain(dve, (kvstat_1, t + 1), (kvnmr_done, t - 1), (kvstd_done, t - 1))
                    nc.vector.bn_aggr(kv_mv[:, par, 0], kv_stat[:, par, 0]).then_inc(kvmv_1, 1)
                    plain(dve, (kvstat_2, t + 1))
                    nc.vector.bn_aggr(kv_mv[:, par, 1], kv_stat[:, par, 1]).then_inc(kvmv_2, 1)
                s, us = t - 1, (u - 1) % 2
                if live(s, NT):
                    wait(dve, kvstd_done, s + 1)
                    wait(dve, vn_done, s - 1)
                    nc.vector.reciprocal(kv_rs[:, us], kv_std[:, us]).then_inc(kvrs_done, 1)
                    wait(dve, kvrs_done, s + 1)
                    nc.vector.scalar_tensor_tensor(kv_nmr[:, us], kv_mv[:, us, :, 0], -1.0, kv_rs[:, us],
                                                   ALU.mult, ALU.mult).then_inc(kvnmr_done, 1)
                    wait(dve, kvnmr_done, s + 1)
                    wait(dve, vn_done, s - 1)
                    nc.vector.tensor_scalar(v_sc[:, us], kv_sc[:, us, :, 1], masks_sb[:, col(s), 1], None,
                                            ALU.mult).then_inc(vsc_done, 1)
                s, us = t - 2, u % 2
                if live(s, NT):
                    wait(dve, kvbeta_done, s + 1)
                    wait(dve, acc_done, s - 1)
                    nc.vector.tensor_scalar(kp_sb[:, us], k_g[:, us], 0.0, EPS_K, ALU.max, ALU.add).then_inc(kp_done, 1)
                    nc.vector.tensor_copy(va_sb[:, us, :, P:VA], masks_sb[:, col(s)].to_broadcast([P, DC, 2])).then_inc(vmask_done, 1)
                s, us = t - 3, (u - 3) % TPB
                par = us % 2
                if live(s, NT):
                    if isinstance(s, int) and s == 0:
                        dve.wait_ge(xq_in, 16)
                    wait(dve, xmv_done, s - 1)
                    nc.vector.bn_stats(x_stat[:, par], xq_sb[:, col(s)].rearrange("p a d -> p (a d)")).then_inc(xstat_done, 1)
                    plain(dve, (xstat_done, s + 1), (xmvcopy_done, s - 1))
                    nc.vector.bn_aggr(x_mv1[:, par], x_stat[:, par]).then_inc(xmv_done, 1)
                    wait(dve, xmv_done, s + 1)
                    nc.vector.tensor_copy(x_mv[:, col(s)].rearrange("p a d -> p (a d)"), x_mv1[:, par]).then_inc(xmvcopy_done, 1)
                if live(s, NT) and us == TPB - 1:
                    wait(dve, acc_done, s + 1)
                    if isinstance(s, int) and s < TPB:
                        dve.wait_ge(vgb_done, 2 * DC)
                    batch = kvbd[:, col(batch_of(s, us))].rearrange("p a c n -> p (a c) n")
                    for c in range(DC):
                        nc.vector.tensor_tensor(kvg_sb[:, c], kvacc_ps[c][:, 0:P], vgamma_sb[:, c], ALU.mult).then_inc(kvg_done, 1)
                        nc.vector.tensor_scalar(batch[:, c, P:KVW], const("heads"), kvacc_ps[c][:, P:P + 1], None,
                                                ALU.mult).then_inc(kvsum_done, 1)
                        wait(dve, kvg_done, (batch_of(s, us)) * DC + c + 1)
                        nc.vector.scalar_tensor_tensor(batch[:, c, 0:P], vbeta_sb[:, c], kvacc_ps[c][:, P + 1:VA], kvg_sb[:, c],
                                                       ALU.mult, ALU.add).then_inc(kvbd_done, 1)
            pass1(dve, step1)

            dve.wait_ge(xstd_done, 1)
            nc.vector.reciprocal(x_rs[:, :], x_std[:, :]).then_inc(xrs_done, 1)
            dve.wait_ge(xrs_done, 1)

            def step2(t, u):
                if live(t, NT):
                    wait(dve, xTps_done, t - 1)
                    nc.vector.tensor_scalar(xn_sb[:, u], xq_sb[:, col(t)].rearrange("p a d -> p (a d)"), x_mv[:, col(t), 0],
                                            x_rs[:, col(t)], ALU.subtract, ALU.mult).then_inc(xn_done, 1)
                s, us = t - 2, u
                if live(s, NT):
                    scales("q", s, us, qn_done)
                s, us = t - 4, u
                if live(s, NT):
                    wait(dve, attps_done, s + 1)
                    wait(dve, att_done, s - 1)
                    both = att_ps[:, 0:DC * KVW].rearrange("p (c n) -> p c n", c=DC)
                    z = z_sb[:, us].rearrange("p (c h) -> p c h", c=DC)
                    nc.vector.tensor_scalar(z, both[:, :, P:KVW], EPS_K, None, ALU.add).then_inc(den_done, 1)
                    wait(dve, den_done, s + 1)
                    nc.vector.reciprocal(z_sb[:, us], z_sb[:, us]).then_inc(z_done, 1)
                    wait(dve, z_done, s + 1)
                    rows = att_sb[:, col(s)].rearrange("p a d -> p (a d)")
                    for c in range(DC):
                        last = nc.vector.tensor_tensor(
                            rows[:, c * P:(c + 1) * P].rearrange("p (h e) -> p h e", h=HPC),
                            both[:, c, 0:P].rearrange("p (h e) -> p h e", h=HPC),
                            z[:, c, :].unsqueeze(2).to_broadcast([P, HPC, DH]), ALU.mult)
                    last.then_inc(att_done, 1)
                s, us = t - 3, (u - 3) % 2
                if live(s, NT):
                    wait(dve, relu_q, (s + 1) * DC)
                    wait(dve, attps_done, s - 1)
                    nc.vector.tensor_scalar(qpT_sb[:, us], qr_sb[:, us], EPS_K, None, ALU.add).then_inc(qpT_done, 1)
                s, us = t - 1, (u - 1) % 2
                if live(s, NT):
                    wait(dve, q_done, s + 1)
                    stats("q", s, us, q_ps[us][:, 0:D])
            pass23(dve, step2, LAG2)
            dve.wait_ge(xb_done, NT)

            def step3(t, u):
                s, us = t - 2, u
                if live(s, NT):
                    scales("o", s, us, on_done)
                s, us = t - 3, (u - 3) % 2
                if live(s, NT):
                    wait(dve, og_done, s + 1)
                    wait(dve, x1_stored[us], (s - us) * 8)
                    wait(dve, x2_done, s - 1)
                    nc.vector.tensor_tensor(x1_sb[:, us], on_sb[:, us], x_sb[:, col(s)].rearrange("p a d -> p (a d)"),
                                            ALU.add).then_inc(x1_done, 1)
                    wait(dve, x1_done, s + 1)
                    stats("r", s, us, x1_sb[:, us])
                s, us = t - 4, u
                if live(s, NT):
                    scales("r", s, us, x2_done)
                    wait(dve, x2_stored[us], (s - us) * 8)
                    wait(dve, x2Tps_done, s - 1)
                    nc.vector.tensor_scalar(x2_sb[:, us], x1_sb[:, us], mv["r"][:, us, 0:1], rs["r"][:, us],
                                            ALU.subtract, ALU.mult).then_inc(x2_done, 1)
                s, us = t - 5, (u - 5) % 2
                if live(s, NT):
                    wait(dve, lgps_done, s + 1)
                    wait(dve, topi_done, s - 1)
                    nc.vector.tensor_copy(lg_sb[:, us], lg_ps[:, 0:E]).then_inc(lg_done, 1)
                    plain(dve, (lg_done, s + 1), (choicev_done, s - 1))
                    nc.vector.max(top_v[:, us], lg_sb[:, us]).then_inc(topv_done, 1)
                    plain(dve, (topv_done, s + 1), (choicei_done, s - 1))
                    nc.vector.max_index(top_i[:, us], top_v[:, us], lg_sb[:, us]).then_inc(topi_done, 1)
                    nc.vector.tensor_copy(choice_v[:, :, col(s)].rearrange("p k a -> p (k a)"), top_v[:, us, 0:TOPK]).then_inc(choicev_done, 1)
                    wait(dve, topi_done, s + 1)
                    nc.vector.tensor_copy(choice_i[:, :, col(s)].rearrange("p k a -> p (k a)"), top_i[:, us, 0:TOPK]).then_inc(choicei_done, 1)
                s, us = t - 1, (u - 1) % 2
                if live(s, NT):
                    wait(dve, o_done, s + 1)
                    stats("o", s, us, o_ps[us][:, 0:D])
            pass23(dve, step3, LAG3)

            steps = [0]

            def chain(ins):
                steps[0] += 1
                ins.then_inc(slot_step, 1)
                dve.wait_ge(slot_step, steps[0])

            tt, ts = nc.vector.tensor_tensor, nc.vector.tensor_scalar
            dve.wait_ge(choicev_done, NT)
            dve.wait_ge(choicei_done, NT)
            experts = const("iota_e").unsqueeze(1)
            for k in range(TOPK):
                chain(tt(onehot[:, k], choice_i[:, k].unsqueeze(2).to_broadcast([P, NT, E]),
                         experts.to_broadcast([P, NT, E]), ALU.is_equal))
            tt(chosen[:, :, :], onehot[:, 0], onehot[:, 1], ALU.add).then_inc(chosen_done, 1)
            tt(gdiff[:, 0], choice_v[:, 1], choice_v[:, 0], ALU.subtract).then_inc(gdiff_done, 1)
            dve.wait_ge(total_done, 1)
            chain(nc.vector.tensor_copy(totT[:, :, :], total_ps[:, 0:NT * E].rearrange("p (t e) -> p e t", e=E)))
            chain(nc.vector.tensor_tensor_scan(incl[:, :, :].rearrange("p e t -> p (e t)"), const("restart"),
                                               totT[:, :, :].rearrange("p e t -> p (e t)"), 0.0, ALU.mult, ALU.add))
            chain(tt(tiles_cmp[:, :, :], incl[:, :, NT - 1:NT].to_broadcast([P, E, NT]),
                     const("fill").unsqueeze(1).to_broadcast([P, E, NT]), ALU.is_gt))
            chain(nc.vector.tensor_reduce(tiles_of[:, :], tiles_cmp[:, :, :], AX.X, ALU.add))
            chain(nc.vector.tensor_tensor_scan(ends[:, :], const("ones")[:, 0:E], tiles_of[:, :], 0.0, ALU.mult, ALU.add))
            chain(tt(starts[:, :], ends[:, :], tiles_of[:, :], ALU.subtract))
            chain(tt(base[:, :, :], incl[:, :, :], totT[:, :, :], ALU.subtract))
            chain(nc.vector.scalar_tensor_tensor(base[:, :, :], starts[:, :].unsqueeze(2).to_broadcast([P, E, NT]), float(P),
                                                 base[:, :, :], ALU.mult, ALU.add))
            dve.wait_ge(within_done, 1)
            chain(tt(pos[:, :, :], within_ps[:, 0:NT * E].rearrange("p (t e) -> p t e", e=E),
                     base[:, :, :].rearrange("p e t -> p t e"), ALU.add))
            for k in range(TOPK):
                chain(tt(picked[:, k * NT:(k + 1) * NT], onehot[:, k], pos[:, :, :], ALU.mult))
            chain(nc.vector.tensor_reduce(dest[:, :], picked[:, :, :], AX.X, ALU.add))
            chain(nc.vector.tensor_copy(dest_i[:, :], dest[:, :]))
            chain(ts(tile_i[:, :], dest_i[:, :], P.bit_length() - 1, None, ALU.logical_shift_right))
            chain(ts(row_i[:, :], dest_i[:, :], P - 1, None, ALU.bitwise_and))
            chain(nc.vector.tensor_copy(tile_f[:, :], tile_i[:, :]))
            chain(nc.vector.tensor_copy(row_f[:, :], row_i[:, :]))
            dve.wait_ge(gexp_done, 1)
            chain(ts(gdiff[:, 2], gdiff[:, 1], 1.0, None, ALU.add))
            chain(nc.vector.reciprocal(gate[:, 0], gdiff[:, 2]))
            chain(tt(gate[:, 1], gate[:, 0], gdiff[:, 1], ALU.mult))
            for k in range(TOPK):
                chain(nc.vector.scalar_tensor_tensor(load_f[:, k * NT:(k + 1) * NT], const("token"), -float(PAD),
                                                     row_f[:, k * NT:(k + 1) * NT], ALU.add, ALU.subtract))
            for k in range(TOPK):
                a, b = k * NT, (k + 1) * NT
                chain(tt(in_row[:, a:b, :], row_f[:, a:b].unsqueeze(2).to_broadcast([P, NT, P]),
                         const("iota_p").unsqueeze(1).to_broadcast([P, NT, P]), ALU.is_equal))
                chain(tt(in_tile[:, a:b, :], tile_f[:, a:b].unsqueeze(2).to_broadcast([P, NT, ST]),
                         const("iota_st").unsqueeze(1).to_broadcast([P, NT, ST]), ALU.is_equal))
                chain(tt(carry[:, a:b, 0, :], in_tile[:, a:b, :], load_f[:, a:b].unsqueeze(2).to_broadcast([P, NT, ST]), ALU.mult))
                tt(carry[:, a:b, 1, :], in_tile[:, a:b, :], gate[:, k].unsqueeze(2).to_broadcast([P, NT, ST]),
                   ALU.mult).then_inc(spread_done, 1)
            chain(tt(exp_cmp[:, :, :], ends[:, :].unsqueeze(1).to_broadcast([P, ST, E]),
                     const("iota_st").unsqueeze(2).to_broadcast([P, ST, E]), ALU.is_le))
            chain(nc.vector.tensor_reduce(exp_f[:, :], exp_cmp[:, :, :], AX.X, ALU.add))
            ts(exp_i[:, :], exp_f[:, :], float(E - 1), None, ALU.min).then_inc(exp_done, 1)
            dve.wait_ge(slots_done, 1)
            chain(ts(slot_f[:, :], slots_ps[:, 0:ST], const("pad_row"), None, ALU.add))
            nc.vector.tensor_copy(slot_row[:, :], slot_f[:, :]).then_inc(slot_done, 1)
            nc.vector.tensor_copy(slot_gate[:, :], slots_ps[:, ST:2 * ST]).then_inc(gate_done, 1)

            def rows_out(j, par):
                wait(dve, gTps_done, j + 1)
                if live(j - 2, ST):
                    wait(dve, hps_done, (j - 2) * 2 + 2)
                nc.vector.tensor_copy(gT_sb[:, par], gT_ps[:, 0:D]).then_inc(gT_done, 1)

            def step4(j, par):
                for half in range(2):
                    wait(dve, hTps_done, j * 2 + half + 1)
                    wait(dve, yps_done, j)
                    nc.vector.tensor_copy(hT_sb[:, half * 512:(half + 1) * 512], hT_ps[half][:, :]).then_inc(hT_done, 1)
                if live(j + 2, ST):
                    rows_out(j + 2, par)
            rows_out(0, 0)
            rows_out(1, 1)
            pass4(dve, step4)


def kernel(x, ctx_1024, mask_BxS2_ff1, L0_xattn_wq, L0_xattn_wk, L0_xattn_wv, L0_xattn_ln_gamma, L0_xattn_ln_beta,
           L0_xattn_dense_w, L0_xattn_dense_b, L0_ffn_gate_w, L0_ffn_w1, L0_ffn_w2):
    import concourse.bacc as bacc
    from concourse.bass_utils import run_bass_kernel_spmd

    def chunked(w):
        return np.asarray(w).reshape(DC, P, -1).transpose(1, 0, 2)

    x = np.asarray(x)
    arrays = {
        "xq": x.reshape(B, NH, TPB, NLT, D).transpose(3, 1, 0, 2, 4).reshape(P, NT, D),
        "xr": x.reshape(B, H, NH, D).transpose(0, 2, 1, 3).reshape(P, NT, D),
        "ctxT": np.asarray(ctx_1024).reshape(NT, P, DC, P).transpose(3, 0, 2, 1),
        "maskT": np.asarray(mask_BxS2_ff1).reshape(NT, P).T,
        "wq": chunked(L0_xattn_wq),
        "wkv": chunked(np.concatenate([L0_xattn_wk, L0_xattn_wv], axis=1)),
        "wd": chunked(L0_xattn_dense_w),
        "gamma": np.asarray(L0_xattn_ln_gamma),
        "beta": np.asarray(L0_xattn_ln_beta),
        "gbT": np.stack([L0_xattn_ln_gamma, L0_xattn_ln_beta]).reshape(2, DC, P).transpose(2, 0, 1),
        "bd": np.asarray(L0_xattn_dense_b).reshape(1, D),
        "gw": chunked(np.asarray(L0_ffn_gate_w).T),
        "w1": np.asarray(L0_ffn_w1).reshape(E, F, DC, P).transpose(3, 0, 2, 1),
        "w2": np.asarray(L0_ffn_w2).reshape(E, D, FC, P).transpose(3, 0, 2, 1),
        "consts": constants(),
    }
    arrays = {f"in_{name}": np.ascontiguousarray(a) for name, a in arrays.items()}
    nc = bacc.Bacc("TRN2", target_bir_lowering=False, num_devices=1)
    args = [nc.dram_tensor(name, a.shape, F32, kind="ExternalInput").ap() for name, a in arrays.items()]
    out = nc.dram_tensor("out", [N + P, D], F32, kind="ExternalOutput").ap()
    build(nc, *args, out)
    result = run_bass_kernel_spmd(nc, [arrays], core_ids=[0])
    rows = result.results[0]["out"][:N].reshape(H, B, NH, D)
    return np.ascontiguousarray(rows.transpose(1, 0, 2, 3)).reshape(B, S, D)
```

```python
from contextlib import ExitStack

import concourse.bass as bass
import numpy as np
from concourse import mybir

F32 = mybir.dt.float32
F16 = mybir.dt.float16
BF16 = mybir.dt.bfloat16
I32 = mybir.dt.int32
U32 = mybir.dt.uint32
ALU = mybir.AluOpType
ACT = mybir.ActivationFunctionType
AX = mybir.AxisListType

P = 128
B, S, D = 4, 512, 256
N = B * S
DC = D // P
H, DH = 16, 16
HPC = P // DH
E, F, TOPK = 8, 1024, 2
FC = F // P
NT = N // P
NH = S // H
NLT = P // NH
TPB = S // P
ST = N * TOPK // P + E - 1
UNIT = D * F // P
VA = P + 2
KVW = P + HPC
NORM1, NORM2 = 2.0 ** 11, 2.0 ** 15
GATE_UP = 2.0 ** 12
PAD = N
EPS_IN, EPS_LN, EPS_K = 1e-5, 1e-6, 1e-6

CONSTS = {}
_at = 0
for _name, _width in [("ident", P), ("tri", P), ("ones", P), ("blocks", P), ("heads", HPC), ("iota_p", P),
                      ("iota_st", ST), ("iota_e", E), ("fill", NT), ("restart", E * NT), ("token", NT),
                      ("pad_row", 1), ("eps_in", 1), ("eps_ln", 1)]:
    CONSTS[_name] = (_at, _at + _width)
    _at += _width
CW = _at


def constants():
    c = np.zeros((P, CW), np.float32)
    p = np.arange(P)

    def put(name, value):
        a, b = CONSTS[name]
        c[:, a:b] = value

    put("ident", np.eye(P))
    put("tri", p[:, None] < p[None, :])
    put("ones", 1.0)
    put("blocks", p[:, None] // DH == p[None, :] // DH)
    put("heads", p[:, None] // DH == np.arange(HPC)[None, :])
    put("iota_p", p[None, :])
    put("iota_st", np.arange(ST)[None, :])
    put("iota_e", np.arange(E)[None, :])
    put("fill", P * np.arange(NT)[None, :])
    put("restart", (np.arange(E * NT) % NT != 0)[None, :])
    put("token", p[:, None] + P * np.arange(NT)[None, :])
    put("pad_row", PAD + 1 + p[:, None])
    put("eps_in", EPS_IN)
    put("eps_ln", EPS_LN)
    return c


def build(nc, xq, xr, ctxT, maskT, wq, wkv, wd, gamma, beta, gbT, bd, gw, w1, w2, consts, out):
    x2_rows = nc.dram_tensor("x2_rows", [N + P, 2 * D], F16).ap()

    with ExitStack() as stack:
        def sb(name, shape, dt=F32):
            return stack.enter_context(nc.sbuf_tensor(name, shape, dt))

        def sem(name):
            return stack.enter_context(nc.semaphore(name))

        bank = [stack.enter_context(nc.psum_tensor(f"bank{i}", [P, 512], F32)) for i in range(8)]

        w_sb = sb("w_sb", [P, 2 * E + 1, UNIT])
        wq_sb = sb("wq_sb", [P, DC, D])
        wkv_sb = sb("wkv_sb", [P, DC, 2 * D])
        ident16 = sb("ident16", [P, P], F16)
        wd_sb = sb("wd_sb", [P, DC, D])
        gw_sb = sb("gw_sb", [P, DC, E])
        gamma_sb = sb("gamma_sb", [P, D])
        beta_sb = sb("beta_sb", [P, D])
        gbT_sb = sb("gbT_sb", [P, 2, DC])
        vgb_sb = sb("vgb_sb", [P, 2, DC, P])
        vgamma_sb, vbeta_sb = vgb_sb[:, 0], vgb_sb[:, 1]
        w_sq = sb("w_sq", [P, 2 * E])
        w_root = sb("w_root", [P, 2 * E])
        w_scale = sb("w_scale", [P, 2 * E])
        unscale = sb("unscale", [P, E])
        bd_sb = sb("bd_sb", [1, D])
        bd_parts = sb("bd_parts", [1, 3, D], BF16)
        bias_rows = sb("bias_rows", [3, D], BF16)
        ones16 = sb("ones16", [3, P], BF16)
        c_sb = sb("c_sb", [P, CW])

        def const(name):
            a, b = CONSTS[name]
            return c_sb[:, a:b]

        ident = const("ident")

        x_sb = sb("x_sb", [P, NT, D])
        mask_sb = sb("mask_sb", [P, NT])
        masks_sb = sb("masks_sb", [P, NT, 2])
        ctx_sb = x_sb[:, 0:TPB, :].rearrange("p t (c n) -> p t c n", c=DC)
        kv_stat = sb("kv_stat", [P, 2, 2, 6])
        kv_mv = sb("kv_mv", [P, 2, 2, 2])
        kv_std = sb("kv_std", [P, 2, 2])
        kv_sc = sb("kv_sc", [P, 2, 2, 2])
        kv_rs, kv_nmr = kv_sc[:, :, 0], kv_sc[:, :, 1]
        v_sc = sb("v_sc", [P, 2, 2])
        work1 = sb("work1", [P, 6 * D + 2 * DC * VA + 224])
        k_n, k_g, kp_sb = (work1[:, i * 2 * D:(i + 1) * 2 * D].rearrange("p (a d) -> p a d", a=2) for i in range(3))
        va_sb = work1[:, 6 * D:6 * D + 2 * DC * VA].rearrange("p (a c n) -> p a c n", a=2, c=DC)
        kvg_sb = sb("kvg_sb", [P, DC, P])
        kvacc_sb = sb("kvacc_sb", [P, DC, VA])
        kvbd = sb("kvbd", [P, B, DC, KVW])

        x_stat = sb("x_stat", [P, 2, 6])
        x_mv1 = sb("x_mv1", [P, TPB, 2])
        x_mv = sb("x_mv", [P, NT, 2])
        x_std = sb("x_std", [P, NT])
        x_rs = sb("x_rs", [P, NT])

        def place(k):
            return w_sb[:, k + 1:k + 3].rearrange("p a (t d) -> p (a t) d", d=D)

        xq_sb = place(E + 2)
        att_sb = place(E + 4)
        heads_sb = place(E + 6)
        work = sb("work", [P, 9, 2, D])
        xn_sb, xT_sb, qn_sb, qr_sb, qpT_sb, head_sb, aT_sb, on_sb, x2T_sb = (work[:, i] for i in range(9))
        squares = work[:, 0:4].rearrange("p i a d -> p (i a d)")
        x1_sb, x2_sb = wkv_sb[:, 0].rearrange("p (a d) -> p a d", a=2), wkv_sb[:, 1].rearrange("p (a d) -> p a d", a=2)
        x2p_sb = vgb_sb[:, :, :, :].rearrange("p a c n -> p a (c n)").bitcast(F16)
        z_sb = sb("z_sb", [P, 2, H])
        stat = {k: sb(f"stat_{k}", [P, 2, 6]) for k in "qor"}
        mv = {k: sb(f"mv_{k}", [P, 2, 2]) for k in "qor"}
        std = {k: sb(f"std_{k}", [P, 2, 1]) for k in "qor"}
        rs = {k: sb(f"rs_{k}", [P, 2, 1]) for k in "qor"}
        nmr = {k: sb(f"nmr_{k}", [P, 2, 1]) for k in "qor"}
        top_v = sb("top_v", [P, 2, 8])
        top_i = sb("top_i", [P, 2, 8], U32)

        carved = [0]

        def carve(*shape):
            size = int(np.prod(shape))
            a = carved[0]
            carved[0] += size
            names = "abc"[:len(shape)]
            spread = " ".join(names)
            return work1[:, a:a + size].rearrange(f"p ({spread}) -> p {spread}", **dict(zip(names, shape)))

        onehot = carve(TOPK * NT, E).rearrange("p (k t) e -> p k t e", k=TOPK)
        choice_v, choice_i = carve(TOPK, NT), carve(TOPK, NT)
        picked = carve(TOPK * NT, E)
        chosen = carve(NT, E)
        totT, incl, tiles_cmp, base = (carve(E, NT) for _ in range(4))
        pos = carve(NT, E)
        exp_cmp = carve(ST, E)
        gdiff = carve(3, NT)
        gate = carve(TOPK, NT)
        tiles_of = carve(E)
        ends = carve(E)
        starts = carve(E)
        dest = carve(TOPK * NT)
        dest_i = carve(TOPK * NT).bitcast(I32)
        tile_i = carve(TOPK * NT).bitcast(I32)
        row_i = carve(TOPK * NT).bitcast(I32)
        tile_f = carve(TOPK * NT)
        row_f = carve(TOPK * NT)
        gate_c = carve(TOPK * NT)
        load = carve(TOPK * NT * 3 // 2).bitcast(F16).rearrange("p (k a) -> p k a", a=3)
        used = work[:, :, :, :].rearrange("p i a d -> p (i a d)").bitcast(F16)
        pairs = TOPK * NT * ST
        in_tile = used[:, 0:pairs].rearrange("p (k s) -> p k s", s=ST)
        carry = used[:, pairs:4 * pairs].rearrange("p (k a s) -> p k a s", a=3, s=ST)
        in_row = x_sb[:, 0:TOPK * NT * P // (2 * D), :].rearrange("p t d -> p (t d)").bitcast(F16).rearrange(
            "p (k r) -> p k r", r=P)
        exp_f = carve(ST)
        exp_i = carve(ST).bitcast(I32)
        slot_f = carve(ST)
        slot_row = carve(ST).bitcast(U32)
        slot_gate = carve(ST)
        slot_scale = carve(ST)

        def lent(a, n, dt=F16):
            return x_sb[:, a:a + 2 * n].rearrange("p (u n) d -> p u (n d)", u=2).bitcast(dt)

        hT_sb, xg_sb, gT_sb, y_sb = lent(0, 2), lent(8, 1), lent(10, 1), lent(12, 1, F32)
        hidden_sb = x_sb[:, 4:8, :].rearrange("p a b -> p (a b)")
        row_sb = sb("row_sb", [P, 2, 1], U32)
        grow_sb = sb("grow_sb", [P, 2, 1], U32)
        zero_sb = sb("zero_sb", [P, D])

        kv_ps, kvacc_ps = bank[0:4], bank[4:6]
        xT_ps, q_ps, qT_ps, att_ps = bank[6], (bank[7], bank[2]), bank[0], bank[1]
        aT_ps, o_ps, x2T_ps, lg_ps = bank[4], (bank[5], bank[1]), bank[2], bank[3]
        within_ps, total_ps, slots_ps = bank[6], bank[7], bank[0]
        h_ps, hT_ps, gT_ps, y_ps = bank[0:2], bank[2:4], bank[4][:, :].bitcast(F16), bank[5:7]
        total_sq = {(0, E): bank[3], (E, 2 * E - 2): bank[6], (2 * E - 2, 2 * E): bank[3]}

        consts_in, wkv_in, ctx_in, x_in = sem("consts_in"), sem("wkv_in"), [sem(f"ctx_in{i}") for i in range(4)], sem("x_in")
        small_in, late_in = sem("small_in"), sem("late_in")
        w1_in, w2_in = [sem(f"w1_in{i}") for i in range(2)], [sem(f"w2_in{i}") for i in range(E)]
        sq_done, sqsum_done, root_done, pow_done, clamp_done, inv_done, scale_done = (
            sem(n) for n in ("sq_done", "sqsum_done", "root_done", "pow_done", "clamp_done", "inv_done", "scale_done"))
        scaled_done = sem("scaled_done")
        whi_done, wlo_done, ident16_done = sem("whi_done"), sem("wlo_done"), sem("ident16_done")
        kv_done, kvstat_1, kvstat_2, kvmv_1, kvmv_2, kvstd_done, kvrs_done, kvnmr_done = (
            sem(n) for n in ("kv_done", "kvstat_1", "kvstat_2", "kvmv_1", "kvmv_2", "kvstd_done", "kvrs_done", "kvnmr_done"))
        kn_done, vn_done, kvgamma_done, kvbeta_done = (sem(n) for n in ("kn_done", "vn_done", "kvgamma_done", "kvbeta_done"))
        kp_done, vmask_done, acc_done, mask2_done = (sem(n) for n in ("kp_done", "vmask_done", "acc_done", "mask2_done"))
        acc_copied = sem("acc_copied")
        kvbd_done, kvsum_done, kvg_done, vsc_done, vgb_done = (
            sem(n) for n in ("kvbd_done", "kvsum_done", "kvg_done", "vsc_done", "vgb_done"))
        xb_done = sem("xb_done")
        xq_in, xstat_done, xmv_done, xmvcopy_done, xstd_done, xrs_done = (
            sem(n) for n in ("xq_in", "xstat_done", "xmv_done", "xmvcopy_done", "xstd_done", "xrs_done"))
        spread_in = [sem(f"spread_in{i}") for i in range(B)]
        xn_done, xTps_done, xT_done, q_done, qn_done, relu_q = (
            sem(n) for n in ("xn_done", "xTps_done", "xT_done", "q_done", "qn_done", "relu_q"))
        qTps_done, qpT_done, attps_done, den_done, z_done, att_done = (
            sem(n) for n in ("qTps_done", "qpT_done", "attps_done", "den_done", "z_done", "att_done"))
        head_done = sem("head_done")
        aTps_done, aT_done, o_done, on_done, og_done = (
            sem(n) for n in ("aTps_done", "aT_done", "o_done", "on_done", "og_done"))
        x1_done, x2_done, x2Tps_done, x2T_done, lgps_done = (
            sem(n) for n in ("x1_done", "x2_done", "x2Tps_done", "x2T_done", "lgps_done"))
        bias_step, bias_in, ones16_done = sem("bias_step"), sem("bias_in"), sem("ones16_done")
        x2hi_done, x2lo_done = sem("x2hi_done"), sem("x2lo_done")
        x1_stored, x2_stored = ([sem(f"{n}{i}") for i in range(2)] for n in ("x1_stored", "x2_stored"))
        topv_done, topi_done, choicev_done, choicei_done = (
            sem(n) for n in ("topv_done", "topi_done", "choicev_done", "choicei_done"))
        stat_done = {k: sem(f"stat_done_{k}") for k in "qor"}
        mv_done = {k: sem(f"mv_done_{k}") for k in "qor"}
        std_done = {k: sem(f"std_done_{k}") for k in "qor"}
        rs_done = {k: sem(f"rs_done_{k}") for k in "qor"}
        nmr_done = {k: sem(f"nmr_done_{k}") for k in "qor"}
        slot_step, chosen_done, within_done, total_done, gdiff_done, gexp_done = (
            sem(n) for n in ("slot_step", "chosen_done", "within_done", "total_done", "gdiff_done", "gexp_done"))
        spread_done, slots_done, exp_done, slot_done, gate_done = (
            sem(n) for n in ("spread_done", "slots_done", "exp_done", "slot_done", "gate_done"))
        zero_done, zero_stored = sem("zero_done"), sem("zero_stored")
        gathered = [sem(f"gathered{i}") for i in range(2)]
        grow_done, row_done, gTps_done, gT_done, hps_done = (
            sem(n) for n in ("grow_done", "row_done", "gTps_done", "gT_done", "hps_done"))
        relu_done, hTps_done = sem("relu_done"), sem("hTps_done")
        hhi_done, hlo_done, yps_done, y_done, added, grow_first = (
            sem(n) for n in ("hhi_done", "hlo_done", "yps_done", "y_done", "added", "grow_first"))

        LAG2, LAG3 = 6, 8
        SMALL, LATE = 3, 5

        def wait(eng, s, count):
            if not isinstance(count, int) or count > 0:
                eng.wait_ge(s, count)

        def plain(eng, *needs):
            eng.wait_ge(consts_in, 16)
            for s, count in needs:
                wait(eng, s, count)

        def live(t, n):
            return not isinstance(t, int) or 0 <= t < n

        def col(t):
            return bass.DynSlice(t, 1)

        def batch_of(t, u):
            return t // TPB if isinstance(t, int) else (t - u) // TPB

        def unit(k):
            return w_sb[:, col(k + 1)].rearrange("p a n -> p (a n)")

        def split(k):
            both = w_sb[:, col(k)].rearrange("p a n -> p (a n)").bitcast(F16)
            return both[:, 0:UNIT], both[:, UNIT:2 * UNIT]

        HALF = UNIT // 2
        CONV2, CONV3 = 3, 9
        SQ3 = CONV3 - 2
        SPLIT = 2 * (2 * E - 2)

        def pass1(eng, step):
            for t in range(TPB):
                step(t, t)
            with eng.Fori(1, B) as b:
                for u in range(TPB):
                    step(b * TPB + u, u)
            for t in range(NT, NT + 4):
                step(t, t % TPB)

        def pass23(eng, step, lag):
            first = lag + 2
            for t in range(first):
                step(t, t % 2)
            with eng.Fori(first // 2, NT // 2) as i:
                for u in range(2):
                    step(i * 2 + u, u)
            for t in range(NT, NT + lag):
                step(t, t % 2)

        def pass4(eng, step):
            for j in range(2):
                step(j, j)
            with eng.Fori(1, (ST - 3) // 2) as i:
                for u in range(2):
                    step(i * 2 + u, u)
            for j in range((ST - 3) // 2 * 2, ST):
                step(j, j % 2)

        block = stack.enter_context(nc.Block())

        @block.sync
        def _(sp):
            sp.dma_start(wkv_sb[:, :, :], wkv).then_inc(wkv_in, 16)
            sp.dma_start(ctx_sb[:, 0], ctxT[:, 0]).then_inc(ctx_in[0], 16)
            sp.dma_start(c_sb[:, :], consts).then_inc(consts_in, 16)
            for u in range(1, TPB):
                sp.dma_start(ctx_sb[:, u], ctxT[:, u]).then_inc(ctx_in[u], 16)
            for dst, src in ((gamma_sb[:, :], gamma.partition_broadcast(P)), (beta_sb[:, :], beta.partition_broadcast(P)),
                             (mask_sb[:, :], maskT)):
                sp.dma_start(dst, src).then_inc(small_in, 16)
            sp.dma_start(xq_sb[:, 0:TPB], xq[:, 0:TPB]).then_inc(xq_in, 16)
            with sp.Fori(1, B) as b:
                for u in range(TPB):
                    t = b * TPB + u
                    sp.wait_ge(kv_done, t - (TPB - 1))
                    sp.dma_start(ctx_sb[:, u], ctxT[:, col(t)].rearrange("p a c n -> p (a c) n")).then_inc(ctx_in[u], 16)
                sp.wait_ge(xq_in, b * 16)
                here = bass.DynSlice(b * TPB, TPB)
                sp.dma_start(xq_sb[:, here], xq[:, here]).then_inc(xq_in, 16)
            for dst, src in ((wq_sb[:, :, :], wq), (gbT_sb[:, :, :], gbT), (wd_sb[:, :, :], wd), (gw_sb[:, :, :], gw),
                             (bd_sb[:, :], bd)):
                sp.dma_start(dst, src).then_inc(late_in, 16)
            sp.wait_ge(zero_done, 1)
            sp.dma_start(x2_rows[N:N + P, :], zero_sb[:, :].bitcast(F16)).then_inc(zero_stored, 16)
            sp.dma_start(out[N:N + P, :], zero_sb[:, :]).then_inc(zero_stored, 16)

            sp.wait_ge(kv_done, NT)
            sp.dma_start(x_sb[:, :, :], xr).then_inc(x_in, 16)

            def spread(b):
                sp.wait_ge(att_done, (b + 1) * TPB)
                for i in range(NLT):
                    sp.dma_start(heads_sb[b * NH:(b + 1) * NH, i::NLT, :],
                                 att_sb[i * NH:(i + 1) * NH, b * TPB:(b + 1) * TPB]).then_inc(spread_in[b], 16)

            for e in (0, 1):
                sp.dma_start(unit(E + e), w2[:, e]).then_inc(w2_in[e], 16)
            sp.wait_ge(bias_step, 5)
            for i in range(3):
                sp.dma_start(bias_rows[i:i + 1, :], bd_parts[:, i]).then_inc(bias_in, 16)
            for b in range(B):
                if b == B - 1:
                    sp.wait_ge(xTps_done, NT)
                    for e in (2, 3):
                        sp.dma_start(unit(E + e), w2[:, e]).then_inc(w2_in[e], 16)
                spread(b)
            for b in range(B):
                sp.wait_ge(spread_in[b], 16 * NLT)
            for e in (4, 5):
                sp.dma_start(unit(E + e), w2[:, e]).then_inc(w2_in[e], 16)

            def step(t, u):
                s, us = t - 4, u
                if live(s, NT):
                    wait(sp, x1_done, s + 1)
                    sp.dma_start(out[bass.DynSlice(s * P, P), :], x1_sb[:, us]).then_inc(x1_stored[us], 16)
                s, us = t - 7, (u - 7) % 2
                if live(s, NT):
                    wait(sp, x2lo_done, s + 1)
                    sp.dma_start(x2_rows[bass.DynSlice(s * P, P), :], x2p_sb[:, us]).then_inc(x2_stored[us], 16)
                if isinstance(t, int) and t == NT + 1:
                    sp.wait_ge(head_done, NT)
                    for e in (6, 7):
                        sp.dma_start(unit(E + e), w2[:, e]).then_inc(w2_in[e], 16)
            pass23(sp, step, LAG3)

        @block.tensor
        def _(pe):
            def transpose(dst, src, chunks, done, eye=ident):
                for c in range(chunks):
                    last = nc.tensor.transpose(dst[:, c * P:(c + 1) * P], src[:, c * P:(c + 1) * P], eye)
                last.then_inc(done, 1)

            def add_squares(a, b):
                pe.wait_ge(sq_done, b + 1)
                nc.tensor.matmul(total_sq[a, b][:, 0:b - a], const("ones"), w_sq[:, a:b],
                                 start=True, stop=True).then_inc(sqsum_done, 1)

            pe.wait_ge(wkv_in, 16)

            def step1(t, u):
                if live(t, NT):
                    wait(pe, ctx_in[u], 16 * ((t - u) // TPB + 1) if isinstance(t, int) else (t - u) * (16 // TPB) + 16)
                    wait(pe, vn_done, t - (TPB - 1))
                    for c in range(DC):
                        last = nc.tensor.matmul(kv_ps[u][:, :], ctx_sb[:, u, c, :], wkv_sb[:, c, :],
                                                start=(c == 0), stop=(c == DC - 1))
                    last.then_inc(kv_done, 1)
                s, us = t - 3, (u - 3) % TPB
                if live(s, NT):
                    wait(pe, vn_done, s + 1)
                    wait(pe, vmask_done, s + 1)
                    wait(pe, kp_done, s + 1)
                    if us == 0:
                        wait(pe, acc_copied, batch_of(s, us) * DC)
                    for c in range(DC):
                        last = nc.tensor.matmul(kvacc_ps[c][:, 0:VA], kp_sb[:, us % 2, c * P:(c + 1) * P],
                                                va_sb[:, us % 2, c, :], start=(us == 0), stop=(us == TPB - 1))
                    last.then_inc(acc_done, 1)
            pass1(pe, step1)

            pe.wait_ge(consts_in, 16)
            pe.wait_ge(late_in, 16 * LATE)

            def step2(t, u):
                s, us = t - 4, u
                if live(s, NT):
                    wait(pe, qn_done, s + 1)
                    wait(pe, relu_q, s * DC)
                    transpose(qT_ps, qn_sb[:, us], DC, qTps_done)
                s, us = t - 1, (u - 1) % 2
                if live(s, NT):
                    if isinstance(s, int) and s == 1:
                        pe.wait_ge(vn_done, NT)
                    wait(pe, xT_done, s + 1)
                    wait(pe, qn_done, s - 1)
                    for c in range(DC):
                        last = nc.tensor.matmul(q_ps[us][:, 0:D], xT_sb[:, us, c * P:(c + 1) * P], wq_sb[:, c, :],
                                                start=(c == 0), stop=(c == DC - 1))
                    last.then_inc(q_done, 1)
                s, us = t - 5, (u - 5) % 2
                if live(s, NT):
                    b = s // TPB
                    wait(pe, kvbd_done, (b + 1) * DC)
                    wait(pe, kvsum_done, (b + 1) * DC)
                    wait(pe, qpT_done, s + 1)
                    wait(pe, att_done, s)
                    batch = kvbd[:, col(b)].rearrange("p a c n -> p (a c) n")
                    for c in range(DC):
                        last = nc.tensor.matmul(att_ps[:, c * KVW:(c + 1) * KVW], qpT_sb[:, us, c * P:(c + 1) * P],
                                                batch[:, c, :], start=True, stop=True)
                    last.then_inc(attps_done, 1)
                if live(t, NT):
                    wait(pe, xn_done, t + 1)
                    wait(pe, xT_done, t)
                    transpose(xT_ps, xn_sb[:, u], DC, xTps_done)
                if isinstance(t, int) and t == CONV2 - 1:
                    add_squares(0, E)
            pass23(pe, step2, LAG2)

            pe.wait_ge(kvbd_done, DC * B)
            pe.wait_ge(ones16_done, 1)
            pe.wait_ge(bias_in, 16 * 3)

            def step3(t, u):
                s, us = t - 6, u
                if live(s, NT):
                    wait(pe, x2_done, s + 1)
                    wait(pe, x2T_done, s)
                    transpose(x2T_ps, x2_sb[:, us], DC, x2Tps_done)
                if live(t, NT):
                    wait(pe, head_done, t + 1)
                    wait(pe, aT_done, t)
                    transpose(aT_ps, head_sb[:, u], DC, aTps_done)
                s, us = t - 7, (u - 7) % 2
                if live(s, NT):
                    wait(pe, x2T_done, s + 1)
                    wait(pe, topi_done, s)
                    for c in range(DC):
                        last = nc.tensor.matmul(lg_ps[:, 0:E], x2T_sb[:, us, c * P:(c + 1) * P], gw_sb[:, c, :],
                                                start=(c == 0), stop=(c == DC - 1))
                    last.then_inc(lgps_done, 1)
                s, us = t - 1, (u - 1) % 2
                if live(s, NT):
                    wait(pe, aT_done, s + 1)
                    wait(pe, on_done, s - 1)
                    for c in range(DC):
                        nc.tensor.matmul(o_ps[us][:, 0:D], aT_sb[:, us, c * P:(c + 1) * P], wd_sb[:, c, :],
                                         start=(c == 0), stop=False)
                    nc.tensor.matmul(o_ps[us][:, 0:D], ones16[:, :], bias_rows[:, :],
                                     start=False, stop=True).then_inc(o_done, 1)
                if isinstance(t, int) and t == CONV3 - 1:
                    add_squares(E, 2 * E - 2)
            pass23(pe, step3, LAG3)

            pe.wait_ge(chosen_done, 1)
            flat = chosen[:, :, :].rearrange("p t e -> p (t e)")
            nc.tensor.matmul(within_ps[:, 0:NT * E], const("tri"), flat, start=True, stop=True).then_inc(within_done, 1)
            nc.tensor.matmul(total_ps[:, 0:NT * E], const("ones"), flat, start=True, stop=True).then_inc(total_done, 1)
            add_squares(2 * E - 2, 2 * E)
            for k in range(TOPK * NT):
                if k % NT == 0:
                    pe.wait_ge(spread_done, k // NT + 1)
                last = nc.tensor.matmul(slots_ps[:, 0:3 * ST], in_row[:, k, :], carry[:, k].rearrange("p a s -> p (a s)"),
                                        start=(k == 0), stop=(k == TOPK * NT - 1))
            last.then_inc(slots_done, 1)

            pe.wait_ge(exp_done, 1)
            pe.wait_ge(slot_done, 1)
            pe.wait_ge(ident16_done, 1)
            pe.wait_ge(wlo_done, 2 * E)

            def rows_T(j, par):
                wait(pe, gathered[par], (j - par) * 8 + 16)
                wait(pe, gT_done, j)
                transpose(gT_ps, xg_sb[:, par], 2 * DC, gTps_done, ident16[:, :])

            def expert(j, layer):
                e = pe.value_load(exp_i[0:1, col(j)], min_val=0, max_val=E - 1)
                return split(layer * E + e)

            def products(dst, parts, first, last):
                (s_hi, s_lo), (m_hi, m_lo) = parts
                nc.tensor.matmul(dst, s_hi, m_hi, start=first, stop=False)
                nc.tensor.matmul(dst, s_hi, m_lo, start=False, stop=False)
                return nc.tensor.matmul(dst, s_lo, m_hi, start=False, stop=last)

            def layer1(j, par):
                w = expert(j, 0)
                wait(pe, gT_done, j + 1)
                for half in range(2):
                    wait(pe, relu_done, (j - 1) * 2 + half + 1)
                    for c in range(DC):
                        last = products(h_ps[half][:, :],
                                        ([gT_sb[:, par, (i * DC + c) * P:(i * DC + c + 1) * P] for i in range(2)],
                                         [part[:, c * F + half * 512:c * F + (half + 1) * 512] for part in w]),
                                        c == 0, c == DC - 1)
                    last.then_inc(hps_done, 1)

            def step4(j, par):
                for half in range(2):
                    wait(pe, relu_done, j * 2 + half + 1)
                    if live(j - 1, ST):
                        wait(pe, hlo_done, (j - 1) * 2 + half + 1)
                    transpose(hT_ps[half], hidden_sb[:, half * 512:(half + 1) * 512], 4, hTps_done)
                if live(j + 1, ST):
                    layer1(j + 1, 1 - par)
                if live(j + 2, ST):
                    rows_T(j + 2, par)
                w = expert(j, 1)
                wait(pe, y_done, j - 1)
                for c in range(FC):
                    if c % 4 == 0:
                        wait(pe, hlo_done, j * 2 + c // 4 + 1)
                    last = products(y_ps[par][:, 0:D],
                                    ([hT_sb[:, part, c * P:(c + 1) * P] for part in range(2)],
                                     [part[:, c * D:(c + 1) * D] for part in w]), c == 0, c == FC - 1)
                last.then_inc(yps_done, 1)
            rows_T(0, 0)
            rows_T(1, 1)
            layer1(0, 0)
            pe.wait_ge(wlo_done, SPLIT + 2)
            pass4(pe, step4)

        @block.scalar
        def _(act):
            def norm(dst, src, r, m, done):
                nc.scalar.activation(dst, src, ACT.Identity, bias=m, scale=r).then_inc(done, 1)

            def root(k, s, us, eps):
                wait(act, mv_done[k], s + 1)
                nc.scalar.activation(std[k][:, us], mv[k][:, us, 1:2], ACT.Sqrt, bias=const(eps)).then_inc(std_done[k], 1)

            def sum_squares(k, before, need, count, dst=squares):
                plain(act, (need, count), (sq_done, before))
                nc.scalar.activation(dst, unit(k), ACT.Square, accum_out=w_sq[:, col(k)]).then_inc(sq_done, 1)

            def roots(a, b, parts):
                act.wait_ge(sqsum_done, parts)
                nc.scalar.activation(w_root[:, a:b], total_sq[a, b][:, 0:b - a], ACT.Sqrt).then_inc(root_done, 1)

            def leading(k, half, count, scaled=False):
                a, b = half * HALF, (half + 1) * HALF
                if scaled:
                    plain(act, (scaled_done, (count + 1) // 2))
                    nc.scalar.copy(split(k)[0][:, a:b], unit(k)[:, a:b]).then_inc(whi_done, 1)
                else:
                    plain(act, (wlo_done, count - half))
                    nc.scalar.activation(split(k)[0][:, a:b], unit(k)[:, a:b], ACT.Copy,
                                         scale=w_scale[:, col(k)]).then_inc(whi_done, 1)

            act.wait_ge(consts_in, 16)

            def step1(t, u):
                par = u % 2
                if live(t, NT):
                    wait(act, kvmv_1, t + 1)
                    wait(act, kvmv_2, t + 1)
                    wait(act, kvrs_done, t - 1)
                    nc.scalar.activation(kv_std[:, par], kv_mv[:, par, :, 1], ACT.Sqrt,
                                         bias=const("eps_ln")).then_inc(kvstd_done, 1)
                s, us = t - 1, (u - 1) % TPB
                par = us % 2
                if live(s, NT):
                    wait(act, kvnmr_done, s + 1)
                    wait(act, kvgamma_done, s - 1)
                    norm(k_n[:, par], kv_ps[us][:, 0:D], kv_rs[:, par, 0:1], kv_nmr[:, par, 0:1], kn_done)
                    wait(act, vsc_done, s + 1)
                    wait(act, acc_done, s - 1)
                    norm(va_sb[:, par, :, 0:P], kv_ps[us][:, D:].rearrange("p (c n) -> p c n", c=DC),
                         v_sc[:, par, 0:1], v_sc[:, par, 1:2], vn_done)
                s, us = t - 3, (u - 3) % TPB
                if live(s, NT) and us == TPB - 1:
                    wait(act, acc_done, s + 1)
                    wait(act, kvbd_done, batch_of(s, us) * DC)
                    for c in range(DC):
                        nc.scalar.copy(kvacc_sb[:, c], kvacc_ps[c][:, 0:VA]).then_inc(acc_copied, 1)
                e, odd = (t - u) // 2 + u // 2, u // 2
                if u % 2 == 0 and live(e - 2, E - 1):
                    sum_squares(e - 2, (t - u - 2) // 2 + odd, w1_in[odd], (e - odd) * 16)
                if live(t, NT):
                    a, b = u % 2 * HALF, (u % 2 + 1) * HALF
                    act.dma_start(unit(e)[:, a:b], w1[:, col(e)].rearrange("p a n -> p (a n)")[:, a:b]).then_inc(w1_in[odd], 16)
            pass1(act, step1)
            act.wait_ge(late_in, 16 * LATE)
            act.wait_ge(xmvcopy_done, B)
            nc.scalar.activation(x_std[:, :], x_mv[:, :, 1], ACT.Sqrt, bias=const("eps_in")).then_inc(xstd_done, 1)

            def step2(t, u):
                s, us = t - 1, (u - 1) % 2
                if live(s, NT):
                    wait(act, xTps_done, s + 1)
                    nc.scalar.copy(xT_sb[:, us], xT_ps[:, 0:D]).then_inc(xT_done, 1)
                s, us = t - 3, (u - 3) % 2
                if live(s, NT):
                    wait(act, nmr_done["q"], s + 1)
                    norm(qn_sb[:, us], q_ps[us][:, 0:D], rs["q"][:, us], nmr["q"][:, us], qn_done)
                s, us = t - 4, u
                if live(s, NT):
                    wait(act, qTps_done, s + 1)
                    wait(act, qpT_done, s - 1)
                    for c in range(DC):
                        nc.scalar.activation(qr_sb[:, us, c * P:(c + 1) * P], qT_ps[:, c * P:(c + 1) * P], ACT.Relu,
                                             bias=gbT_sb[:, 1, c:c + 1], scale=gbT_sb[:, 0, c:c + 1]).then_inc(relu_q, 1)
                s, us = t - 2, u
                if live(s, NT):
                    root("q", s, us, "eps_ln")
                if isinstance(t, int) and t == CONV2 - 1:
                    sum_squares(E - 1, E, w1_in[1], 16 * E, w_sb[:, 0])
                    roots(0, E, 1)
                if isinstance(t, int) and t == CONV2:
                    act.wait_ge(scale_done, 1)
                i, half = t - CONV2, (u - CONV2) % 2
                if live(i, 2 * E):
                    leading((i - half) // 2, half, i, scaled=half == 1)
            pass23(act, step2, LAG2)
            act.wait_ge(wlo_done, 2 * E)
            for e in range(4):
                sum_squares(E + e, E + e + 1, w2_in[e], 16, w_sb[:, E])

            def step3(t, u):
                s, us = t - 1, (u - 1) % 2
                if live(s, NT):
                    wait(act, aTps_done, s + 1)
                    nc.scalar.copy(aT_sb[:, us], aT_ps[:, 0:D]).then_inc(aT_done, 1)
                s, us = t - 3, (u - 3) % 2
                if live(s, NT):
                    wait(act, nmr_done["o"], s + 1)
                    norm(on_sb[:, us], o_ps[us][:, 0:D], rs["o"][:, us], nmr["o"][:, us], on_done)
                s, us = t - 6, u
                if live(s, NT):
                    wait(act, x2_done, s + 1)
                    wait(act, x2_stored[us], (s - us) * 8)
                    nc.scalar.copy(x2p_sb[:, us, 0:D], x2_sb[:, us]).then_inc(x2hi_done, 1)
                    wait(act, x2Tps_done, s + 1)
                    wait(act, lgps_done, s - 1)
                    nc.scalar.copy(x2T_sb[:, us], x2T_ps[:, 0:D]).then_inc(x2T_done, 1)
                s, us = t - 2, u
                if live(s, NT):
                    root("o", s, us, "eps_ln")
                s, us = t - 4, u
                if live(s, NT):
                    root("r", s, us, "eps_in")
                if isinstance(t, int) and SQ3 <= t < CONV3:
                    e = 4 + t - SQ3
                    sum_squares(E + e, E + e + 1, w2_in[e], 16)
                if isinstance(t, int) and t == CONV3 - 1:
                    roots(E, 2 * E - 2, 2)
                    act.wait_ge(scale_done, 2)
                i, half = t - CONV3, (u - CONV3) % 2
                if live(i, 2 * E - 4):
                    leading(E + (i - half) // 2, half, 2 * E + i)
            pass23(act, step3, LAG3)

            act.wait_ge(gdiff_done, 1)
            nc.scalar.activation(gdiff[:, 1], gdiff[:, 0], ACT.Exp).then_inc(gexp_done, 1)
            act.wait_ge(wlo_done, SPLIT)
            for e in (E - 2, E - 1):
                sum_squares(E + e, E + e + 1, w2_in[e], 16, w_sb[:, 2 * E - 2])
            roots(2 * E - 2, 2 * E, 3)
            act.wait_ge(scale_done, 3)
            for i, k in enumerate((2 * E - 2, 2 * E - 1)):
                nc.scalar.activation(unit(k), unit(k), ACT.Copy, scale=w_scale[:, k:k + 1]).then_inc(scaled_done, 1)
                act.wait_ge(scaled_done, E + i + 1)
                act.wait_ge(wlo_done, SPLIT + i)
                nc.scalar.copy(split(k)[0], unit(k)).then_inc(whi_done, 1)
            act.wait_ge(slots_done, 1)
            act.wait_ge(gate_done, 1)

            def step4(j, par):
                for half in range(2):
                    wait(act, hps_done, j * 2 + half + 1)
                    if live(j - 1, ST):
                        wait(act, hTps_done, (j - 1) * 2 + half + 1)
                    nc.scalar.activation(hidden_sb[:, half * 512:(half + 1) * 512], h_ps[half][:, :], ACT.Relu).then_inc(relu_done, 1)
                for half in range(2):
                    wait(act, hTps_done, j * 2 + half + 1)
                    if live(j - 1, ST):
                        wait(act, yps_done, j)
                    nc.scalar.copy(hT_sb[:, 0, half * 512:(half + 1) * 512], hT_ps[half][:, :]).then_inc(hhi_done, 1)
                if live(j - 1, ST):
                    gated(j - 1, 1 - par)

            def gated(j, par):
                wait(act, yps_done, j + 1)
                wait(act, added, (j - 1) * 16)
                nc.scalar.mul(y_sb[:, par], y_ps[par][:, 0:D], slot_gate[:, col(j)]).then_inc(y_done, 1)
            pass4(act, step4)
            gated(ST - 1, (ST - 1) % 2)

        @block.gpsimd
        def _(pool):
            nc.gpsimd.memset(zero_sb[:, :], 0.0).then_inc(zero_done, 1)
            pool.wait_ge(small_in, 16 * SMALL)

            def step1(t, u):
                s, us = t - 1, (u - 1) % 2
                if live(s, NT):
                    wait(pool, kn_done, s + 1)
                    wait(pool, kp_done, s - 1)
                    nc.gpsimd.tensor_tensor(k_g[:, us], k_n[:, us], gamma_sb[:, :], ALU.mult).then_inc(kvgamma_done, 1)
                    wait(pool, kvgamma_done, s + 1)
                    nc.gpsimd.tensor_tensor(k_g[:, us], k_g[:, us], beta_sb[:, :], ALU.add).then_inc(kvbeta_done, 1)
            pass1(pool, step1)

            nc.gpsimd.memset(ones16[:, :], 1.0).then_inc(ones16_done, 1)
            pool.wait_ge(late_in, 16 * LATE)
            for i in range(3):
                wait(pool, bias_step, 2 * i)
                nc.gpsimd.tensor_copy(bd_parts[:, i], bd_sb[:, :]).then_inc(bias_step, 1)
                if i < 2:
                    pool.wait_ge(bias_step, 2 * i + 1)
                    nc.gpsimd.tensor_tensor(bd_sb[:, :], bd_sb[:, :], bd_parts[:, i], ALU.subtract).then_inc(bias_step, 1)
            pool.wait_ge(x_in, 16)

            def step2(t, u):
                if live(t, NT):
                    row = x_sb[:, col(t)].rearrange("p a d -> p (a d)")
                    nc.gpsimd.tensor_tensor(row, row, beta_sb[:, :], ALU.add).then_inc(xb_done, 1)
                i, half = t - CONV2 + 1, (u - CONV2 + 1) % 2
                if isinstance(i, int) and i == 0:
                    pool.wait_ge(scale_done, 1)
                if half == 0 and live(i, 2 * E):
                    raw = unit(i // 2)[:, HALF:]
                    nc.gpsimd.tensor_tensor(raw, raw, w_scale[:, col(i // 2)].to_broadcast([P, HALF]), ALU.mult).then_inc(scaled_done, 1)
                i, half = t - CONV2 - 1, (u - CONV2 - 1) % 2
                if half == 1 and live(i, 2 * E):
                    k = (i - half) // 2
                    plain(pool, (whi_done, i + 1))
                    hi, lo = split(k)
                    nc.gpsimd.tensor_tensor(lo[:, HALF:], unit(k)[:, HALF:], hi[:, HALF:], ALU.subtract).then_inc(wlo_done, 1)
            pass23(pool, step2, LAG2)

            for b in range(B):
                pool.wait_ge(spread_in[b], 16 * NLT)

            def step3(t, u):
                if live(t, NT):
                    wait(pool, aTps_done, t - 1)
                    nc.gpsimd.tensor_copy(head_sb[:, u].rearrange("p (n e) -> p n e", e=DH),
                                          heads_sb[:, :, bass.DynSlice(t * DH, DH)]).then_inc(head_done, 1)
                s, us = t - 3, (u - 3) % 2
                if live(s, NT):
                    wait(pool, on_done, s + 1)
                    nc.gpsimd.tensor_tensor(on_sb[:, us], on_sb[:, us], gamma_sb[:, :], ALU.mult).then_inc(og_done, 1)
                s, us = t - 6, u
                if live(s, NT):
                    wait(pool, x2hi_done, s + 1)
                    nc.gpsimd.tensor_tensor(x2p_sb[:, us, D:], x2_sb[:, us], x2p_sb[:, us, 0:D], ALU.subtract).then_inc(x2lo_done, 1)
            pass23(pool, step3, LAG3)

            for i, k in enumerate((2 * E - 2, 2 * E - 1)):
                pool.wait_ge(whi_done, SPLIT + i + 1)
                hi, lo = split(k)
                nc.gpsimd.tensor_tensor(lo, unit(k), hi, ALU.subtract).then_inc(wlo_done, 1)

            pool.wait_ge(slot_done, 1)
            for par in range(2):
                pool.wait_ge(x2_stored[par], 16 * NT // 2)
                pool.wait_ge(x1_stored[par], 16 * NT // 2)
            pool.wait_ge(zero_stored, 32)

            def gather(j, par, copied, before):
                nc.gpsimd.tensor_copy(grow_sb[:, par], slot_row[:, col(j)]).then_inc(copied, 1)
                plain(pool, (copied, before))
                nc.gpsimd.indirect_dma_start(
                    out=xg_sb[:, par], out_offset=None, in_=x2_rows,
                    in_offset=bass.IndirectOffsetOnAxis(ap=grow_sb[:, par], axis=0)).then_inc(gathered[par], 16)

            def step4(j, par):
                if live(j + 3, ST):
                    wait(pool, gathered[1 - par], (j + 1) * 8 + 8 + 8 * par)
                    wait(pool, gTps_done, j + 2)
                    gather(j + 3, 1 - par, grow_done, j + 1)
                wait(pool, added, j * 16)
                nc.gpsimd.tensor_copy(row_sb[:, par], slot_row[:, col(j)]).then_inc(row_done, 1)
                plain(pool, (row_done, j + 1), (y_done, j + 1))
                nc.gpsimd.indirect_dma_start(
                    out=out, out_offset=bass.IndirectOffsetOnAxis(ap=row_sb[:, par], axis=0),
                    in_=y_sb[:, par], in_offset=None, compute_op=ALU.add).then_inc(added, 16)
            gather(0, 0, grow_first, 1)
            gather(1, 1, grow_first, 2)
            pool.wait_ge(gTps_done, 1)
            pool.wait_ge(gathered[0], 16)
            gather(2, 0, grow_first, 3)
            pass4(pool, step4)
            pool.wait_ge(added, ST * 16)

        @block.vector
        def _(dve):
            def stats(k, s, us, src):
                nc.vector.bn_stats(stat[k][:, us], src).then_inc(stat_done[k], 1)
                plain(dve, (stat_done[k], s + 1))
                nc.vector.bn_aggr(mv[k][:, us], stat[k][:, us]).then_inc(mv_done[k], 1)

            def inverse(k, s, us, used):
                wait(dve, std_done[k], s + 1)
                if used is not None:
                    wait(dve, used, s - 1)
                nc.vector.reciprocal(rs[k][:, us], std[k][:, us]).then_inc(rs_done[k], 1)

            def shift(k, s, us):
                wait(dve, rs_done[k], s + 1)
                nc.vector.scalar_tensor_tensor(nmr[k][:, us], mv[k][:, us, 0:1], -1.0, rs[k][:, us],
                                               ALU.mult, ALU.mult).then_inc(nmr_done[k], 1)

            def scales(a, b, parts, norm):
                bits = w_root[:, a:b].bitcast(I32)
                dve.wait_ge(root_done, parts)
                nc.vector.tensor_scalar(bits, bits, 0x7F800000, None, ALU.bitwise_and).then_inc(pow_done, 1)
                dve.wait_ge(pow_done, parts)
                nc.vector.tensor_scalar(w_root[:, a:b], w_root[:, a:b], 2.0 ** -60, None, ALU.max).then_inc(clamp_done, 1)
                dve.wait_ge(clamp_done, parts)
                nc.vector.reciprocal(w_scale[:, a:b], w_root[:, a:b]).then_inc(inv_done, 1)
                dve.wait_ge(inv_done, parts)
                nc.vector.tensor_scalar(w_scale[:, a:b], w_scale[:, a:b], norm / 2, None, ALU.mult).then_inc(scale_done, 1)

            def rest(k, a, b, count):
                wait(dve, whi_done, count + 1)
                hi, lo = split(k)
                nc.vector.scalar_tensor_tensor(lo[:, a:b], unit(k)[:, a:b], w_scale[:, col(k)], hi[:, a:b],
                                               ALU.mult, ALU.subtract).then_inc(wlo_done, 1)

            dve.wait_ge(consts_in, 16)
            nc.vector.tensor_copy(ident16[:, :], ident).then_inc(ident16_done, 1)
            nc.vector.memset(w_sq[:, :], 0.0).then_inc(sq_done, 1)
            dve.wait_ge(small_in, 16 * SMALL)
            nc.vector.tensor_copy(masks_sb[:, :, 0], mask_sb[:, :]).then_inc(mask2_done, 1)
            nc.vector.tensor_tensor(masks_sb[:, :, 1], mask_sb[:, :], mask_sb[:, :], ALU.mult).then_inc(mask2_done, 1)
            for c in range(DC):
                for dst, src in ((vgamma_sb, gamma_sb), (vbeta_sb, beta_sb)):
                    nc.vector.tensor_tensor(dst[:, c], src[:, c * P:(c + 1) * P], const("blocks"), ALU.mult).then_inc(vgb_done, 1)
            dve.wait_ge(mask2_done, 2)

            def step1(t, u):
                par = u % 2
                r, ur = t - 1, (u - 1) % 2
                if live(t, NT):
                    wait(dve, kv_done, t + 1)
                    nc.vector.bn_stats(kv_stat[:, par, 0], kv_ps[u][:, 0:D]).then_inc(kvstat_1, 1)
                    nc.vector.bn_stats(kv_stat[:, par, 1], kv_ps[u][:, D:]).then_inc(kvstat_2, 1)
                    plain(dve, (kvstat_1, t + 1))
                    nc.vector.bn_aggr(kv_mv[:, par, 0], kv_stat[:, par, 0]).then_inc(kvmv_1, 1)
                if live(r, NT):
                    wait(dve, kvstd_done, r + 1)
                    wait(dve, vn_done, r - 1)
                    nc.vector.reciprocal(kv_rs[:, ur], kv_std[:, ur]).then_inc(kvrs_done, 1)
                if live(t, NT):
                    plain(dve, (kvstat_2, t + 1))
                    nc.vector.bn_aggr(kv_mv[:, par, 1], kv_stat[:, par, 1]).then_inc(kvmv_2, 1)
                if live(r, NT):
                    wait(dve, kvrs_done, r + 1)
                    nc.vector.scalar_tensor_tensor(kv_nmr[:, ur], kv_mv[:, ur, :, 0], -1.0, kv_rs[:, ur],
                                                   ALU.mult, ALU.mult).then_inc(kvnmr_done, 1)
                s, us = t - 2, u % 2
                if live(s, NT):
                    wait(dve, kvbeta_done, s + 1)
                    wait(dve, acc_done, s - 1)
                    nc.vector.tensor_scalar(kp_sb[:, us], k_g[:, us], 0.0, EPS_K, ALU.max, ALU.add).then_inc(kp_done, 1)
                if live(r, NT):
                    wait(dve, kvnmr_done, r + 1)
                    nc.vector.tensor_scalar(v_sc[:, ur], kv_sc[:, ur, :, 1], masks_sb[:, col(r), 1], None,
                                            ALU.mult).then_inc(vsc_done, 1)
                q, uq = t - 3, (u - 3) % TPB
                if live(q, NT):
                    if uq == 0:
                        wait(dve, xq_in, 16 * (q // TPB) + 16)
                    if uq == 0:
                        wait(dve, xmvcopy_done, q // TPB)
                    nc.vector.bn_stats(x_stat[:, uq % 2], xq_sb[:, col(q)].rearrange("p a d -> p (a d)")).then_inc(xstat_done, 1)
                if live(s, NT):
                    nc.vector.tensor_copy(va_sb[:, us, :, P:VA], masks_sb[:, col(s)].to_broadcast([P, DC, 2])).then_inc(vmask_done, 1)
                if live(q, NT):
                    plain(dve, (xstat_done, q + 1))
                    nc.vector.bn_aggr(x_mv1[:, uq], x_stat[:, uq % 2]).then_inc(xmv_done, 1)
                s, us = q, uq
                if live(s, NT) and us == TPB - 1:
                    wait(dve, xmv_done, s + 1)
                    nc.vector.tensor_copy(x_mv[:, bass.DynSlice(s - us, TPB)].rearrange("p a d -> p (a d)"),
                                          x_mv1[:, :, :].rearrange("p a d -> p (a d)")).then_inc(xmvcopy_done, 1)
                s, us = t - 4, u
                if live(s, NT) and us == TPB - 1:
                    wait(dve, acc_copied, (batch_of(s, us) + 1) * DC)
                    if isinstance(s, int) and s < TPB:
                        dve.wait_ge(vgb_done, 2 * DC)
                    batch = kvbd[:, col(batch_of(s, us))].rearrange("p a c n -> p (a c) n")
                    for c in range(DC):
                        nc.vector.tensor_tensor(kvg_sb[:, c], kvacc_sb[:, c, 0:P], vgamma_sb[:, c], ALU.mult).then_inc(kvg_done, 1)
                        nc.vector.tensor_scalar(batch[:, c, P:KVW], const("heads"), kvacc_sb[:, c, P:P + 1], None,
                                                ALU.mult).then_inc(kvsum_done, 1)
                        wait(dve, kvg_done, (batch_of(s, us)) * DC + c + 1)
                        nc.vector.scalar_tensor_tensor(batch[:, c, 0:P], vbeta_sb[:, c], kvacc_sb[:, c, P + 1:VA], kvg_sb[:, c],
                                                       ALU.mult, ALU.add).then_inc(kvbd_done, 1)
            pass1(dve, step1)

            dve.wait_ge(xstd_done, 1)
            nc.vector.reciprocal(x_rs[:, :], x_std[:, :]).then_inc(xrs_done, 1)
            dve.wait_ge(xrs_done, 1)

            def step2(t, u):
                r, ur = t - 3, (u - 3) % 2
                if live(r, NT):
                    inverse("q", r, ur, qn_done)
                s, us = t - 5, (u - 5) % 2
                if live(s, NT):
                    wait(dve, relu_q, (s + 1) * DC)
                    nc.vector.tensor_scalar(qpT_sb[:, us], qr_sb[:, us], EPS_K, None, ALU.add).then_inc(qpT_done, 1)
                s, us = t - 6, u
                if live(s, NT):
                    wait(dve, attps_done, s + 1)
                    both = att_ps[:, 0:DC * KVW].rearrange("p (c n) -> p c n", c=DC)
                    z = z_sb[:, us].rearrange("p (c h) -> p c h", c=DC)
                    nc.vector.tensor_scalar(z, both[:, :, P:KVW], EPS_K, None, ALU.add).then_inc(den_done, 1)
                if live(r, NT):
                    shift("q", r, ur)
                if live(s, NT):
                    wait(dve, den_done, s + 1)
                    nc.vector.reciprocal(z_sb[:, us], z_sb[:, us]).then_inc(z_done, 1)
                if live(t, NT):
                    wait(dve, xTps_done, t - 1)
                    nc.vector.tensor_scalar(xn_sb[:, u], xq_sb[:, col(t)].rearrange("p a d -> p (a d)"), x_mv[:, col(t), 0],
                                            x_rs[:, col(t)], ALU.subtract, ALU.mult).then_inc(xn_done, 1)
                if live(s, NT):
                    wait(dve, z_done, s + 1)
                    rows = att_sb[:, col(s)].rearrange("p a d -> p (a d)")
                    for c in range(DC):
                        last = nc.vector.tensor_tensor(
                            rows[:, c * P:(c + 1) * P].rearrange("p (h e) -> p h e", h=HPC),
                            both[:, c, 0:P].rearrange("p (h e) -> p h e", h=HPC),
                            z[:, c, :].unsqueeze(2).to_broadcast([P, HPC, DH]), ALU.mult)
                    last.then_inc(att_done, 1)
                s, us = t - 2, u
                if live(s, NT):
                    wait(dve, q_done, s + 1)
                    stats("q", s, us, q_ps[us][:, 0:D])
                if isinstance(t, int) and t == CONV2:
                    scales(0, E, 1, NORM1)
                i, half = t - CONV2 - 1, (u - CONV2 - 1) % 2
                if half == 0 and live(i, 2 * E):
                    rest((i - half) // 2, 0, HALF, i)
            pass23(dve, step2, LAG2)
            dve.wait_ge(xb_done, NT)

            def step3(t, u):
                s, us = t - 8, u
                if live(s, NT):
                    wait(dve, lgps_done, s + 1)
                    if us == 0:
                        wait(dve, choicev_done, s // 2)
                        wait(dve, choicei_done, s // 2)
                r, ur = t - 3, (u - 3) % 2
                s, us = t - 5, (u - 5) % 2
                if live(r, NT):
                    inverse("o", r, ur, None)
                if live(s, NT):
                    inverse("r", s, us, None)
                if live(r, NT):
                    shift("o", r, ur)
                if live(s, NT):
                    wait(dve, rs_done["r"], s + 1)
                    wait(dve, x2lo_done, s - 1)
                    wait(dve, x2Tps_done, s - 1)
                    nc.vector.tensor_scalar(x2_sb[:, us], x1_sb[:, us], mv["r"][:, us, 0:1], rs["r"][:, us],
                                            ALU.subtract, ALU.mult).then_inc(x2_done, 1)
                s, us = t - 8, u
                if live(s, NT):
                    plain(dve)
                    nc.vector.max(top_v[:, us], lg_ps[:, 0:E]).then_inc(topv_done, 1)
                s, us = t - 4, u
                if live(s, NT):
                    wait(dve, og_done, s + 1)
                    wait(dve, x1_stored[us], (s - us) * 8)
                    nc.vector.tensor_tensor(x1_sb[:, us], on_sb[:, us], x_sb[:, col(s)].rearrange("p a d -> p (a d)"),
                                            ALU.add).then_inc(x1_done, 1)
                s, us = t - 2, u
                if live(s, NT):
                    wait(dve, o_done, s + 1)
                    stats("o", s, us, o_ps[us][:, 0:D])
                s, us = t - 8, u
                if live(s, NT):
                    plain(dve, (topv_done, s + 1))
                    nc.vector.max_index(top_i[:, us], top_v[:, us], lg_ps[:, 0:E]).then_inc(topi_done, 1)
                s, us = t - 4, u
                if live(s, NT):
                    wait(dve, x1_done, s + 1)
                    stats("r", s, us, x1_sb[:, us])
                s, us = t - 8, u
                if live(s, NT) and us == 1:
                    pair = bass.DynSlice(s - 1, 2)
                    nc.vector.tensor_copy(choice_v[:, :, pair], top_v[:, :, 0:TOPK].rearrange("p t k -> p k t")).then_inc(choicev_done, 1)
                    wait(dve, topi_done, s + 1)
                    nc.vector.tensor_copy(choice_i[:, :, pair], top_i[:, :, 0:TOPK].rearrange("p t k -> p k t")).then_inc(choicei_done, 1)
                if isinstance(t, int) and t == CONV3 - 1:
                    scales(E, 2 * E - 2, 2, NORM2)
                i, half = t - CONV3 - 1, (u - CONV3 - 1) % 2
                if live(i, 2 * E - 4):
                    rest(E + (i - half) // 2, half * HALF, (half + 1) * HALF, 2 * E + i)
            pass23(dve, step3, LAG3)

            steps = [0]

            def chain(ins):
                steps[0] += 1
                ins.then_inc(slot_step, 1)
                dve.wait_ge(slot_step, steps[0])

            tt, ts = nc.vector.tensor_tensor, nc.vector.tensor_scalar
            dve.wait_ge(choicev_done, NT // 2)
            dve.wait_ge(choicei_done, NT // 2)
            experts = const("iota_e").unsqueeze(1)
            for k in range(TOPK):
                chain(tt(onehot[:, k], choice_i[:, k].unsqueeze(2).to_broadcast([P, NT, E]),
                         experts.to_broadcast([P, NT, E]), ALU.is_equal))
            tt(chosen[:, :, :], onehot[:, 0], onehot[:, 1], ALU.add).then_inc(chosen_done, 1)
            tt(gdiff[:, 0], choice_v[:, 1], choice_v[:, 0], ALU.subtract).then_inc(gdiff_done, 1)
            dve.wait_ge(total_done, 1)
            chain(nc.vector.tensor_copy(totT[:, :, :], total_ps[:, 0:NT * E].rearrange("p (t e) -> p e t", e=E)))
            chain(nc.vector.tensor_tensor_scan(incl[:, :, :].rearrange("p e t -> p (e t)"), const("restart"),
                                               totT[:, :, :].rearrange("p e t -> p (e t)"), 0.0, ALU.mult, ALU.add))
            chain(tt(tiles_cmp[:, :, :], incl[:, :, NT - 1:NT].to_broadcast([P, E, NT]),
                     const("fill").unsqueeze(1).to_broadcast([P, E, NT]), ALU.is_gt))
            chain(nc.vector.tensor_reduce(tiles_of[:, :], tiles_cmp[:, :, :], AX.X, ALU.add))
            chain(nc.vector.tensor_tensor_scan(ends[:, :], const("ones")[:, 0:E], tiles_of[:, :], 0.0, ALU.mult, ALU.add))
            chain(tt(starts[:, :], ends[:, :], tiles_of[:, :], ALU.subtract))
            chain(tt(base[:, :, :], incl[:, :, :], totT[:, :, :], ALU.subtract))
            chain(nc.vector.scalar_tensor_tensor(base[:, :, :], starts[:, :].unsqueeze(2).to_broadcast([P, E, NT]), float(P),
                                                 base[:, :, :], ALU.mult, ALU.add))
            dve.wait_ge(within_done, 1)
            chain(tt(pos[:, :, :], within_ps[:, 0:NT * E].rearrange("p (t e) -> p t e", e=E),
                     base[:, :, :].rearrange("p e t -> p t e"), ALU.add))
            for k in range(TOPK):
                chain(tt(picked[:, k * NT:(k + 1) * NT], onehot[:, k], pos[:, :, :], ALU.mult))
            chain(nc.vector.tensor_reduce(dest[:, :], picked[:, :, :], AX.X, ALU.add))
            chain(nc.vector.tensor_copy(dest_i[:, :], dest[:, :]))
            chain(ts(tile_i[:, :], dest_i[:, :], P.bit_length() - 1, None, ALU.logical_shift_right))
            chain(ts(row_i[:, :], dest_i[:, :], P - 1, None, ALU.bitwise_and))
            chain(nc.vector.tensor_copy(tile_f[:, :], tile_i[:, :]))
            chain(nc.vector.tensor_copy(row_f[:, :], row_i[:, :]))
            dve.wait_ge(gexp_done, 1)
            chain(ts(gdiff[:, 2], gdiff[:, 1], 1.0, None, ALU.add))
            chain(nc.vector.reciprocal(gate[:, 0], gdiff[:, 2]))
            chain(tt(gate[:, 1], gate[:, 0], gdiff[:, 1], ALU.mult))
            for k in range(TOPK):
                a, b = k * NT, (k + 1) * NT
                chain(ts(load[:, a:b, 0], const("token"), 1.0, None, ALU.add))
            chain(ts(gate_c[:, :], gate[:, :, :].rearrange("p k t -> p (k t)"), GATE_UP, None, ALU.mult))
            chain(nc.vector.tensor_copy(load[:, :, 1], gate_c[:, :]))
            chain(tt(load[:, :, 2], gate_c[:, :], load[:, :, 1], ALU.subtract))
            scales(2 * E - 2, 2 * E, 3, NORM2)
            for k in range(TOPK):
                a, b = k * NT, (k + 1) * NT
                chain(tt(in_row[:, a:b, :], row_f[:, a:b].unsqueeze(2).to_broadcast([P, NT, P]),
                         const("iota_p").unsqueeze(1).to_broadcast([P, NT, P]), ALU.is_equal))
                chain(tt(in_tile[:, a:b, :], tile_f[:, a:b].unsqueeze(2).to_broadcast([P, NT, ST]),
                         const("iota_st").unsqueeze(1).to_broadcast([P, NT, ST]), ALU.is_equal))
                tt(carry[:, a:b], in_tile[:, a:b, :].unsqueeze(2).to_broadcast([P, NT, 3, ST]),
                   load[:, a:b, :].unsqueeze(3).to_broadcast([P, NT, 3, ST]), ALU.mult).then_inc(spread_done, 1)
            chain(tt(exp_cmp[:, :, :], ends[:, :].unsqueeze(1).to_broadcast([P, ST, E]),
                     const("iota_st").unsqueeze(2).to_broadcast([P, ST, E]), ALU.is_le))
            chain(nc.vector.tensor_reduce(exp_f[:, :], exp_cmp[:, :, :], AX.X, ALU.add))
            chain(ts(exp_f[:, :], exp_f[:, :], float(E - 1), None, ALU.min))
            nc.vector.tensor_copy(exp_i[:, :], exp_f[:, :]).then_inc(exp_done, 1)
            dve.wait_ge(slots_done, 1)
            chain(ts(slot_f[:, :], slots_ps[:, 0:ST], 0.0, const("pad_row"), ALU.is_equal, ALU.mult))
            chain(nc.vector.scalar_tensor_tensor(slot_f[:, :], slots_ps[:, 0:ST], -1.0, slot_f[:, :], ALU.add, ALU.add))
            nc.vector.tensor_copy(slot_row[:, :], slot_f[:, :]).then_inc(slot_done, 1)
            chain(nc.vector.scalar_tensor_tensor(unscale[:, :], w_root[:, 0:E], 4.0 / (NORM1 * NORM2 * GATE_UP), w_root[:, E:2 * E],
                                                 ALU.mult, ALU.mult))
            chain(tt(exp_cmp[:, :, :], exp_f[:, :].unsqueeze(2).to_broadcast([P, ST, E]),
                     const("iota_e").unsqueeze(1).to_broadcast([P, ST, E]), ALU.is_equal))
            chain(tt(exp_cmp[:, :, :], exp_cmp[:, :, :], unscale[:, :].unsqueeze(1).to_broadcast([P, ST, E]), ALU.mult))
            chain(nc.vector.tensor_reduce(slot_scale[:, :], exp_cmp[:, :, :], AX.X, ALU.add))
            chain(nc.vector.tensor_copy(slot_gate[:, :], slots_ps[:, ST:2 * ST]))
            chain(tt(slot_gate[:, :], slot_gate[:, :], slots_ps[:, 2 * ST:3 * ST], ALU.add))
            tt(slot_gate[:, :], slot_gate[:, :], slot_scale[:, :], ALU.mult).then_inc(gate_done, 1)

            def rows_out(j, par):
                wait(dve, gTps_done, j + 1)
                if live(j - 2, ST):
                    wait(dve, hps_done, (j - 2) * 2 + 2)
                nc.vector.tensor_copy(gT_sb[:, par], gT_ps[:, 0:2 * D]).then_inc(gT_done, 1)

            def step4(j, par):
                for half in range(2):
                    a, b = half * 512, (half + 1) * 512
                    wait(dve, hhi_done, j * 2 + half + 1)
                    nc.vector.tensor_tensor(hT_sb[:, 1, a:b], hT_ps[half][:, :], hT_sb[:, 0, a:b], ALU.subtract).then_inc(hlo_done, 1)
                if live(j + 2, ST):
                    rows_out(j + 2, par)
            rows_out(0, 0)
            rows_out(1, 1)
            pass4(dve, step4)


def kernel(x, ctx_1024, mask_BxS2_ff1, L0_xattn_wq, L0_xattn_wk, L0_xattn_wv, L0_xattn_ln_gamma, L0_xattn_ln_beta,
           L0_xattn_dense_w, L0_xattn_dense_b, L0_ffn_gate_w, L0_ffn_w1, L0_ffn_w2):
    import concourse.bacc as bacc
    from concourse.bass_utils import run_bass_kernel_spmd

    def chunked(w):
        return np.asarray(w).reshape(DC, P, -1).transpose(1, 0, 2)

    x = np.asarray(x)
    arrays = {
        "xq": x.reshape(B, NH, TPB, NLT, D).transpose(3, 1, 0, 2, 4).reshape(P, NT, D),
        "xr": x.reshape(B, H, NH, D).transpose(0, 2, 1, 3).reshape(P, NT, D),
        "ctxT": np.asarray(ctx_1024).reshape(NT, P, DC, P).transpose(3, 0, 2, 1),
        "maskT": np.asarray(mask_BxS2_ff1).reshape(NT, P).T,
        "wq": chunked(L0_xattn_wq),
        "wkv": chunked(np.concatenate([L0_xattn_wk, L0_xattn_wv], axis=1)),
        "wd": chunked(L0_xattn_dense_w),
        "gamma": np.asarray(L0_xattn_ln_gamma),
        "beta": np.asarray(L0_xattn_ln_beta),
        "gbT": np.stack([L0_xattn_ln_gamma, L0_xattn_ln_beta]).reshape(2, DC, P).transpose(2, 0, 1),
        "bd": np.asarray(L0_xattn_dense_b).reshape(1, D),
        "gw": chunked(np.asarray(L0_ffn_gate_w).T),
        "w1": np.asarray(L0_ffn_w1).reshape(E, F, DC, P).transpose(3, 0, 2, 1).reshape(P, E, UNIT),
        "w2": np.asarray(L0_ffn_w2).reshape(E, D, FC, P).transpose(3, 0, 2, 1).reshape(P, E, UNIT),
        "consts": constants(),
    }
    arrays = {f"in_{name}": np.ascontiguousarray(a) for name, a in arrays.items()}
    nc = bacc.Bacc("TRN2", target_bir_lowering=False, num_devices=1)
    args = [nc.dram_tensor(name, a.shape, F32, kind="ExternalInput").ap() for name, a in arrays.items()]
    out = nc.dram_tensor("out", [N + P, D], F32, kind="ExternalOutput").ap()
    build(nc, *args, out)
    result = run_bass_kernel_spmd(nc, [arrays], core_ids=[0])
    rows = result.results[0]["out"][:N].reshape(H, B, NH, D)
    return np.ascontiguousarray(rows.transpose(1, 0, 2, 3)).reshape(B, S, D)
```
